# Optimizing a Trainium2 kernel written in Bass

```python
import numpy as np
import jax
import jax.numpy as jnp

def _softmax(x, axis=-1):
    return jax.nn.softmax(x, axis=axis)

def _gelu(x):
    return jax.nn.gelu(x, approximate=True)

def _silu(x):
    return jax.nn.silu(x)

def _sigmoid(x):
    return jax.nn.sigmoid(x)

def _layernorm(x, axis=-1, eps=1e-05):
    m = jnp.mean(x, axis=axis, keepdims=True)
    v = jnp.var(x, axis=axis, keepdims=True)
    return (x - m) / jnp.sqrt(v + eps)

def _scatter_add(tgt, idx, src, axis=0):
    return tgt.at[idx].add(src)

def _segment_sum(src, seg, n):
    return jax.ops.segment_sum(src, seg, n)
kernel_name = 'mk_xattn_seq_d4_seqx_r4_67b0c2'

def setup_inputs(seed: int=0):
    np.random.seed(seed)
    _w = jnp.asarray

    def _rec_inputs():
        import jax
        import jax.numpy as jnp
        _rk = jax.random.key(seed)
        x = 7.22e-05 + 1 * jax.random.normal(jax.random.fold_in(_rk, 1), (32, 128, 1024), jnp.float32)
        _lenS = 128 - jax.random.randint(jax.random.fold_in(_rk, 7), (32,), 0, max(1, 128 // 4) + 1, jnp.int32)
        _lenS2 = 128 - jax.random.randint(jax.random.fold_in(_rk, 8), (32,), 0, max(1, 128 // 4) + 1, jnp.int32)
        _ctx_4096P = jax.random.normal(jax.random.fold_in(_rk, 11), (32, 16, 1024), jnp.float32)
        _ctx_4096c = jax.random.dirichlet(jax.random.fold_in(_rk, 511), 0.3 * jnp.ones((16,), jnp.float32), (32, 128))
        _ctx_4096t = jnp.einsum('bsk,bkd->bsd', _ctx_4096c, _ctx_4096P)
        _ctx_4096t = _ctx_4096t * jax.lax.rsqrt(jnp.mean(jnp.square(_ctx_4096t)) + 1e-12) * 0.953939
        ctx_4096 = 4.13588e-05 + 0.999923 * (_ctx_4096t + 0.3 * jax.random.normal(jax.random.fold_in(_rk, 611), (32, 128, 1024), jnp.float32))
        _validS = jnp.arange(128)[None, :] < _lenS[:, None]
        _validS2 = jnp.arange(128)[None, :] < _lenS2[:, None]
        _causal = jnp.tril(jnp.ones((128, 128), dtype=bool))
        mask_Bx1x4096_ff1 = jnp.where(jnp.ones((32, 1, 1024), dtype=bool), 1.0, 0.0).astype(jnp.float32)
        return (x, ctx_4096, mask_Bx1x4096_ff1)
    x, ctx_4096, mask_Bx1x4096_ff1 = _rec_inputs()

    def _L0_xattn_setup():
        import jax, jax.numpy as jnp
        import numpy as np
        NUM_HEADS = 8
        CHUNK = 64
        EPS = 1e-05
        NEG = -1000000000.0

        def _chunk_attn(q, k, v, masks, W_in, b_in, W_out, b_out):
            N, C, T = q.shape
            H, Dh = (NUM_HEADS, C // NUM_HEADS)
            nc = T // CHUNK
            Wq, Wk, Wv = jnp.split(W_in, 3, axis=0)
            bq, bk, bv = jnp.split(b_in, 3, axis=0)

            def proj(t, W, b):
                t = t.transpose(0, 2, 1) @ W.T + b
                return t.reshape(N, nc, CHUNK, H, Dh)
            qh = proj(q, Wq, bq)
            kh = proj(k, Wk, bk)
            vh = proj(v, Wv, bv)
            scale = 1.0 / jnp.sqrt(jnp.asarray(Dh, q.dtype))
            scores = jnp.einsum('bnqhd,bnkhd->bnhqk', qh, kh) * scale
            km = masks[:, 0, :].reshape(N, nc, CHUNK)
            scores = scores + jnp.where(km[:, :, None, None, :] > 0, 0.0, NEG)
            attn = jax.nn.softmax(scores, axis=-1)
            out = jnp.einsum('bnhqk,bnkhd->bnqhd', attn, vh).reshape(N, T, C)
            out = out @ W_out.T + b_out
            out = out.transpose(0, 2, 1) * masks
            return out
        key = jax.random.key(seed)
        ks = jax.random.split(key, 8)
        N, C, T = (4, 128, 1024)
        x = jax.random.normal(ks[0], (N, C, T), dtype=jnp.float32)
        q = jax.random.normal(ks[1], (N, C, T), dtype=jnp.float32)
        k = jax.random.normal(ks[2], (N, C, T), dtype=jnp.float32)
        v = jax.random.normal(ks[3], (N, C, T), dtype=jnp.float32)
        masks = jnp.ones((N, 1, T), dtype=jnp.float32)
        s = 1.0 / np.sqrt(C)
        W_in = jax.random.normal(ks[4], (3 * C, C), dtype=jnp.float32) * s
        b_in = jnp.zeros((3 * C,), dtype=jnp.float32)
        W_out = jax.random.normal(ks[5], (C, C), dtype=jnp.float32) * s
        b_out = jnp.zeros((C,), dtype=jnp.float32)
        return {'x': x, 'q': q, 'k': k, 'v': v, 'masks': masks, 'W_in': W_in, 'b_in': b_in, 'W_out': W_out, 'b_out': b_out}
    _L0_xattn_all = _L0_xattn_setup()
    _L0_xattn_in = {k: v for k, v in _L0_xattn_all.items() if k in ('W_in', 'b_in', 'W_out', 'b_out')}
    del _L0_xattn_all

    def _L1_xattn_setup():
        import jax, jax.numpy as jnp
        import numpy as np
        NUM_HEADS = 8
        CHUNK = 64
        EPS = 1e-05
        NEG = -1000000000.0

        def _chunk_attn(q, k, v, masks, W_in, b_in, W_out, b_out):
            N, C, T = q.shape
            H, Dh = (NUM_HEADS, C // NUM_HEADS)
            nc = T // CHUNK
            Wq, Wk, Wv = jnp.split(W_in, 3, axis=0)
            bq, bk, bv = jnp.split(b_in, 3, axis=0)

            def proj(t, W, b):
                t = t.transpose(0, 2, 1) @ W.T + b
                return t.reshape(N, nc, CHUNK, H, Dh)
            qh = proj(q, Wq, bq)
            kh = proj(k, Wk, bk)
            vh = proj(v, Wv, bv)
            scale = 1.0 / jnp.sqrt(jnp.asarray(Dh, q.dtype))
            scores = jnp.einsum('bnqhd,bnkhd->bnhqk', qh, kh) * scale
            km = masks[:, 0, :].reshape(N, nc, CHUNK)
            scores = scores + jnp.where(km[:, :, None, None, :] > 0, 0.0, NEG)
            attn = jax.nn.softmax(scores, axis=-1)
            out = jnp.einsum('bnhqk,bnkhd->bnqhd', attn, vh).reshape(N, T, C)
            out = out @ W_out.T + b_out
            out = out.transpose(0, 2, 1) * masks
            return out
        key = jax.random.key(seed)
        ks = jax.random.split(key, 8)
        N, C, T = (4, 128, 1024)
        x = jax.random.normal(ks[0], (N, C, T), dtype=jnp.float32)
        q = jax.random.normal(ks[1], (N, C, T), dtype=jnp.float32)
        k = jax.random.normal(ks[2], (N, C, T), dtype=jnp.float32)
        v = jax.random.normal(ks[3], (N, C, T), dtype=jnp.float32)
        masks = jnp.ones((N, 1, T), dtype=jnp.float32)
        s = 1.0 / np.sqrt(C)
        W_in = jax.random.normal(ks[4], (3 * C, C), dtype=jnp.float32) * s
        b_in = jnp.zeros((3 * C,), dtype=jnp.float32)
        W_out = jax.random.normal(ks[5], (C, C), dtype=jnp.float32) * s
        b_out = jnp.zeros((C,), dtype=jnp.float32)
        return {'x': x, 'q': q, 'k': k, 'v': v, 'masks': masks, 'W_in': W_in, 'b_in': b_in, 'W_out': W_out, 'b_out': b_out}
    _L1_xattn_all = _L1_xattn_setup()
    _L1_xattn_in = {k: v for k, v in _L1_xattn_all.items() if k in ('W_in', 'b_in', 'W_out', 'b_out')}
    del _L1_xattn_all

    def _L2_xattn_setup():
        import jax, jax.numpy as jnp
        import numpy as np
        B, N, C, K = (8, 1024, 64, 30)
        EPS_BN = 1e-05
        TINY = 1e-20

        def _knn(p, k):
            xx = jnp.sum(p * p, axis=1)
            pd = 2.0 * jnp.einsum('bdn,bdm->bnm', p, p) - xx[:, :, None] - xx[:, None, :]
            return jax.lax.top_k(pd, k)[1]

        def _bn(h, g, b):
            mu = jnp.mean(h, axis=(0, 1, 2), keepdims=True)
            var = jnp.var(h, axis=(0, 1, 2), keepdims=True)
            return (h - mu) * jax.lax.rsqrt(var + EPS_BN) * g + b

        def _forward(x_loc, x, W1, g1, b1, W2, g2, b2, W3, g3, b3, k):
            Bsz = x.shape[0]
            idx = _knn(x_loc, k)
            bidx = jnp.arange(Bsz)[:, None, None]
            pts = x_loc.transpose(0, 2, 1)
            rel = pts[bidx, idx] - pts[:, :, None, :]
            xr, yr, zr = (rel[..., 0], rel[..., 1], rel[..., 2])
            sxy2 = xr * xr + yr * yr
            r2 = sxy2 + zr * zr
            rho = jnp.sqrt(jnp.maximum(r2, TINY))
            sxy = jnp.sqrt(jnp.maximum(sxy2, TINY))
            deg_r = r2 < TINY
            deg_p = sxy2 < TINY
            theta = jnp.arctan2(jnp.where(deg_r, 0.0, zr), jnp.where(deg_r, 1.0, sxy))
            phi = jnp.arctan2(jnp.where(deg_p, 0.0, yr), jnp.where(deg_p, 1.0, xr))
            sph = jnp.stack([rho, theta, phi], axis=-1)
            feat = jnp.concatenate([sph, sph - jnp.mean(sph, axis=-1, keepdims=True)], axis=-1)
            lrelu = lambda h: jax.nn.leaky_relu(h, 0.2)
            h = lrelu(_bn(feat @ W1.T, g1, b1))
            h = lrelu(_bn(h @ W2.T, g2, b2))
            h = lrelu(_bn(h @ W3.T, g3, b3))
            att = jax.nn.softmax(h[..., 0], axis=-1)
            xk = x.transpose(0, 2, 1)[bidx, idx]
            agg = jnp.einsum('bnkc,bnk->bnc', xk, att)
            return x + agg.transpose(0, 2, 1)
        key = jax.random.key(seed)
        ks = jax.random.split(key, 12)
        return {'x_loc': jax.random.normal(ks[0], (B, 3, N), jnp.float32), 'x': jax.random.normal(ks[1], (B, C, N), jnp.float32), 'W1': jax.random.normal(ks[2], (6, 6), jnp.float32) * 0.4, 'g1': 1.0 + 0.1 * jax.random.normal(ks[3], (6,), jnp.float32), 'b1': 0.1 * jax.random.normal(ks[4], (6,), jnp.float32), 'W2': jax.random.normal(ks[5], (3, 6), jnp.float32) * 0.4, 'g2': 1.0 + 0.1 * jax.random.normal(ks[6], (3,), jnp.float32), 'b2': 0.1 * jax.random.normal(ks[7], (3,), jnp.float32), 'W3': jax.random.normal(ks[8], (1, 3), jnp.float32) * 0.4, 'g3': 1.0 + 0.1 * jax.random.normal(ks[9], (1,), jnp.float32), 'b3': 0.1 * jax.random.normal(ks[10], (1,), jnp.float32), 'k': K}
    _L2_xattn_all = _L2_xattn_setup()
    _L2_xattn_in = {k: v for k, v in _L2_xattn_all.items() if k in ('W1', 'g1', 'b1', 'W2', 'g2', 'b2', 'W3', 'g3', 'b3')}
    del _L2_xattn_all

    def _L3_xattn_setup():
        import jax, jax.numpy as jnp
        import numpy as np
        NUM_HEADS = 8
        CHUNK = 64
        EPS = 1e-05
        NEG = -1000000000.0

        def _chunk_attn(q, k, v, masks, W_in, b_in, W_out, b_out):
            N, C, T = q.shape
            H, Dh = (NUM_HEADS, C // NUM_HEADS)
            nc = T // CHUNK
            Wq, Wk, Wv = jnp.split(W_in, 3, axis=0)
            bq, bk, bv = jnp.split(b_in, 3, axis=0)

            def proj(t, W, b):
                t = t.transpose(0, 2, 1) @ W.T + b
                return t.reshape(N, nc, CHUNK, H, Dh)
            qh = proj(q, Wq, bq)
            kh = proj(k, Wk, bk)
            vh = proj(v, Wv, bv)
            scale = 1.0 / jnp.sqrt(jnp.asarray(Dh, q.dtype))
            scores = jnp.einsum('bnqhd,bnkhd->bnhqk', qh, kh) * scale
            km = masks[:, 0, :].reshape(N, nc, CHUNK)
            scores = scores + jnp.where(km[:, :, None, None, :] > 0, 0.0, NEG)
            attn = jax.nn.softmax(scores, axis=-1)
            out = jnp.einsum('bnhqk,bnkhd->bnqhd', attn, vh).reshape(N, T, C)
            out = out @ W_out.T + b_out
            out = out.transpose(0, 2, 1) * masks
            return out
        key = jax.random.key(seed)
        ks = jax.random.split(key, 8)
        N, C, T = (4, 128, 1024)
        x = jax.random.normal(ks[0], (N, C, T), dtype=jnp.float32)
        q = jax.random.normal(ks[1], (N, C, T), dtype=jnp.float32)
        k = jax.random.normal(ks[2], (N, C, T), dtype=jnp.float32)
        v = jax.random.normal(ks[3], (N, C, T), dtype=jnp.float32)
        masks = jnp.ones((N, 1, T), dtype=jnp.float32)
        s = 1.0 / np.sqrt(C)
        W_in = jax.random.normal(ks[4], (3 * C, C), dtype=jnp.float32) * s
        b_in = jnp.zeros((3 * C,), dtype=jnp.float32)
        W_out = jax.random.normal(ks[5], (C, C), dtype=jnp.float32) * s
        b_out = jnp.zeros((C,), dtype=jnp.float32)
        return {'x': x, 'q': q, 'k': k, 'v': v, 'masks': masks, 'W_in': W_in, 'b_in': b_in, 'W_out': W_out, 'b_out': b_out}
    _L3_xattn_all = _L3_xattn_setup()
    _L3_xattn_in = {k: v for k, v in _L3_xattn_all.items() if k in ('W_in', 'b_in', 'W_out', 'b_out')}
    del _L3_xattn_all
    return {'x': x, 'ctx_4096': ctx_4096, 'mask_Bx1x4096_ff1': mask_Bx1x4096_ff1, 'L0_xattn_W_in': _L0_xattn_in['W_in'], 'L0_xattn_b_in': _L0_xattn_in['b_in'], 'L0_xattn_W_out': _L0_xattn_in['W_out'], 'L0_xattn_b_out': _L0_xattn_in['b_out'], 'L1_xattn_W_in': _L1_xattn_in['W_in'], 'L1_xattn_b_in': _L1_xattn_in['b_in'], 'L1_xattn_W_out': _L1_xattn_in['W_out'], 'L1_xattn_b_out': _L1_xattn_in['b_out'], 'L2_xattn_W1': _L2_xattn_in['W1'], 'L2_xattn_g1': _L2_xattn_in['g1'], 'L2_xattn_b1': _L2_xattn_in['b1'], 'L2_xattn_W2': _L2_xattn_in['W2'], 'L2_xattn_g2': _L2_xattn_in['g2'], 'L2_xattn_b2': _L2_xattn_in['b2'], 'L2_xattn_W3': _L2_xattn_in['W3'], 'L2_xattn_g3': _L2_xattn_in['g3'], 'L2_xattn_b3': _L2_xattn_in['b3'], 'L3_xattn_W_in': _L3_xattn_in['W_in'], 'L3_xattn_b_in': _L3_xattn_in['b_in'], 'L3_xattn_W_out': _L3_xattn_in['W_out'], 'L3_xattn_b_out': _L3_xattn_in['b_out']}

def reference(x, ctx_4096, mask_Bx1x4096_ff1, L0_xattn_W_in, L0_xattn_b_in, L0_xattn_W_out, L0_xattn_b_out, L1_xattn_W_in, L1_xattn_b_in, L1_xattn_W_out, L1_xattn_b_out, L2_xattn_W1, L2_xattn_g1, L2_xattn_b1, L2_xattn_W2, L2_xattn_g2, L2_xattn_b2, L2_xattn_W3, L2_xattn_g3, L2_xattn_b3, L3_xattn_W_in, L3_xattn_b_in, L3_xattn_W_out, L3_xattn_b_out):
    import jax
    import jax.numpy as jnp

    def _L0_xattn_ref(x, q, k, v, masks, W_in, b_in, W_out, b_out):
        import jax, jax.numpy as jnp
        import numpy as np
        NUM_HEADS = 8
        CHUNK = 64
        EPS = 1e-05
        NEG = -1000000000.0

        def _chunk_attn(q, k, v, masks, W_in, b_in, W_out, b_out):
            N, C, T = q.shape
            H, Dh = (NUM_HEADS, C // NUM_HEADS)
            nc = T // CHUNK
            Wq, Wk, Wv = jnp.split(W_in, 3, axis=0)
            bq, bk, bv = jnp.split(b_in, 3, axis=0)

            def proj(t, W, b):
                t = t.transpose(0, 2, 1) @ W.T + b
                return t.reshape(N, nc, CHUNK, H, Dh)
            qh = proj(q, Wq, bq)
            kh = proj(k, Wk, bk)
            vh = proj(v, Wv, bv)
            scale = 1.0 / jnp.sqrt(jnp.asarray(Dh, q.dtype))
            scores = jnp.einsum('bnqhd,bnkhd->bnhqk', qh, kh) * scale
            km = masks[:, 0, :].reshape(N, nc, CHUNK)
            scores = scores + jnp.where(km[:, :, None, None, :] > 0, 0.0, NEG)
            attn = jax.nn.softmax(scores, axis=-1)
            out = jnp.einsum('bnhqk,bnkhd->bnqhd', attn, vh).reshape(N, T, C)
            out = out @ W_out.T + b_out
            out = out.transpose(0, 2, 1) * masks
            return out
        out = _chunk_attn(q, k, v, masks, W_in, b_in, W_out, b_out) + x
        mu = jnp.mean(out, axis=2, keepdims=True)
        var = jnp.mean(jnp.square(out - mu), axis=2, keepdims=True)
        return (out - mu) * jax.lax.rsqrt(var + EPS)

    def _L1_xattn_ref(x, q, k, v, masks, W_in, b_in, W_out, b_out):
        import jax, jax.numpy as jnp
        import numpy as np
        NUM_HEADS = 8
        CHUNK = 64
        EPS = 1e-05
        NEG = -1000000000.0

        def _chunk_attn(q, k, v, masks, W_in, b_in, W_out, b_out):
            N, C, T = q.shape
            H, Dh = (NUM_HEADS, C // NUM_HEADS)
            nc = T // CHUNK
            Wq, Wk, Wv = jnp.split(W_in, 3, axis=0)
            bq, bk, bv = jnp.split(b_in, 3, axis=0)

            def proj(t, W, b):
                t = t.transpose(0, 2, 1) @ W.T + b
                return t.reshape(N, nc, CHUNK, H, Dh)
            qh = proj(q, Wq, bq)
            kh = proj(k, Wk, bk)
            vh = proj(v, Wv, bv)
            scale = 1.0 / jnp.sqrt(jnp.asarray(Dh, q.dtype))
            scores = jnp.einsum('bnqhd,bnkhd->bnhqk', qh, kh) * scale
            km = masks[:, 0, :].reshape(N, nc, CHUNK)
            scores = scores + jnp.where(km[:, :, None, None, :] > 0, 0.0, NEG)
            attn = jax.nn.softmax(scores, axis=-1)
            out = jnp.einsum('bnhqk,bnkhd->bnqhd', attn, vh).reshape(N, T, C)
            out = out @ W_out.T + b_out
            out = out.transpose(0, 2, 1) * masks
            return out
        out = _chunk_attn(q, k, v, masks, W_in, b_in, W_out, b_out) + x
        mu = jnp.mean(out, axis=2, keepdims=True)
        var = jnp.mean(jnp.square(out - mu), axis=2, keepdims=True)
        return (out - mu) * jax.lax.rsqrt(var + EPS)

    def _L2_xattn_ref(x_loc, x, W1, g1, b1, W2, g2, b2, W3, g3, b3, k):
        import jax, jax.numpy as jnp
        import numpy as np
        B, N, C, K = (8, 1024, 64, 30)
        EPS_BN = 1e-05
        TINY = 1e-20

        def _knn(p, k):
            xx = jnp.sum(p * p, axis=1)
            pd = 2.0 * jnp.einsum('bdn,bdm->bnm', p, p) - xx[:, :, None] - xx[:, None, :]
            return jax.lax.top_k(pd, k)[1]

        def _bn(h, g, b):
            mu = jnp.mean(h, axis=(0, 1, 2), keepdims=True)
            var = jnp.var(h, axis=(0, 1, 2), keepdims=True)
            return (h - mu) * jax.lax.rsqrt(var + EPS_BN) * g + b

        def _forward(x_loc, x, W1, g1, b1, W2, g2, b2, W3, g3, b3, k):
            Bsz = x.shape[0]
            idx = _knn(x_loc, k)
            bidx = jnp.arange(Bsz)[:, None, None]
            pts = x_loc.transpose(0, 2, 1)
            rel = pts[bidx, idx] - pts[:, :, None, :]
            xr, yr, zr = (rel[..., 0], rel[..., 1], rel[..., 2])
            sxy2 = xr * xr + yr * yr
            r2 = sxy2 + zr * zr
            rho = jnp.sqrt(jnp.maximum(r2, TINY))
            sxy = jnp.sqrt(jnp.maximum(sxy2, TINY))
            deg_r = r2 < TINY
            deg_p = sxy2 < TINY
            theta = jnp.arctan2(jnp.where(deg_r, 0.0, zr), jnp.where(deg_r, 1.0, sxy))
            phi = jnp.arctan2(jnp.where(deg_p, 0.0, yr), jnp.where(deg_p, 1.0, xr))
            sph = jnp.stack([rho, theta, phi], axis=-1)
            feat = jnp.concatenate([sph, sph - jnp.mean(sph, axis=-1, keepdims=True)], axis=-1)
            lrelu = lambda h: jax.nn.leaky_relu(h, 0.2)
            h = lrelu(_bn(feat @ W1.T, g1, b1))
            h = lrelu(_bn(h @ W2.T, g2, b2))
            h = lrelu(_bn(h @ W3.T, g3, b3))
            att = jax.nn.softmax(h[..., 0], axis=-1)
            xk = x.transpose(0, 2, 1)[bidx, idx]
            agg = jnp.einsum('bnkc,bnk->bnc', xk, att)
            return x + agg.transpose(0, 2, 1)
        return _forward(x_loc, x, W1, g1, b1, W2, g2, b2, W3, g3, b3, k)

    def _L3_xattn_ref(x, q, k, v, masks, W_in, b_in, W_out, b_out):
        import jax, jax.numpy as jnp
        import numpy as np
        NUM_HEADS = 8
        CHUNK = 64
        EPS = 1e-05
        NEG = -1000000000.0

        def _chunk_attn(q, k, v, masks, W_in, b_in, W_out, b_out):
            N, C, T = q.shape
            H, Dh = (NUM_HEADS, C // NUM_HEADS)
            nc = T // CHUNK
            Wq, Wk, Wv = jnp.split(W_in, 3, axis=0)
            bq, bk, bv = jnp.split(b_in, 3, axis=0)

            def proj(t, W, b):
                t = t.transpose(0, 2, 1) @ W.T + b
                return t.reshape(N, nc, CHUNK, H, Dh)
            qh = proj(q, Wq, bq)
            kh = proj(k, Wk, bk)
            vh = proj(v, Wv, bv)
            scale = 1.0 / jnp.sqrt(jnp.asarray(Dh, q.dtype))
            scores = jnp.einsum('bnqhd,bnkhd->bnhqk', qh, kh) * scale
            km = masks[:, 0, :].reshape(N, nc, CHUNK)
            scores = scores + jnp.where(km[:, :, None, None, :] > 0, 0.0, NEG)
            attn = jax.nn.softmax(scores, axis=-1)
            out = jnp.einsum('bnhqk,bnkhd->bnqhd', attn, vh).reshape(N, T, C)
            out = out @ W_out.T + b_out
            out = out.transpose(0, 2, 1) * masks
            return out
        out = _chunk_attn(q, k, v, masks, W_in, b_in, W_out, b_out) + x
        mu = jnp.mean(out, axis=2, keepdims=True)
        var = jnp.mean(jnp.square(out - mu), axis=2, keepdims=True)
        return (out - mu) * jax.lax.rsqrt(var + EPS)
    x = _L0_xattn_ref(x, ctx_4096, ctx_4096, ctx_4096, mask_Bx1x4096_ff1, L0_xattn_W_in, L0_xattn_b_in, L0_xattn_W_out, L0_xattn_b_out)
    x = _L1_xattn_ref(x, ctx_4096, ctx_4096, ctx_4096, mask_Bx1x4096_ff1, L1_xattn_W_in, L1_xattn_b_in, L1_xattn_W_out, L1_xattn_b_out)
    x = _L2_xattn_ref(ctx_4096, x, L2_xattn_W1, L2_xattn_g1, L2_xattn_b1, L2_xattn_W2, L2_xattn_g2, L2_xattn_b2, L2_xattn_W3, L2_xattn_g3, L2_xattn_b3, 30)
    x = _L3_xattn_ref(x, ctx_4096, ctx_4096, ctx_4096, mask_Bx1x4096_ff1, L3_xattn_W_in, L3_xattn_b_in, L3_xattn_W_out, L3_xattn_b_out)
    return x

_drawn_inputs = setup_inputs


def setup_inputs(seed=0):
    import zlib

    import numpy as np

    out = dict(_drawn_inputs(seed))
    spreads = {'L0_xattn_b_in': (0.0, 0.445),
     'L0_xattn_b_out': (0.0, 0.642),
     'L1_xattn_b_in': (0.0, 0.445),
     'L1_xattn_b_out': (0.0, 0.584),
     'L3_xattn_b_in': (0.0, 0.346),
     'L3_xattn_b_out': (0.0, 0.617)}
    factors = {'L2_xattn_g1': 8.0,
     'L2_xattn_b1': 8.0,
     'L2_xattn_W2': 2.895,
     'L2_xattn_g2': 8.0,
     'L2_xattn_b2': 8.0,
     'L2_xattn_W3': 5.961}
    for name, (base, spread) in spreads.items():
        noise = np.random.default_rng([zlib.crc32(name.encode()), seed]).standard_normal(out[name].shape)
        drawn = base * np.exp(spread * noise) if base else spread * noise
        out[name] = jnp.asarray(drawn.astype(out[name].dtype))
    for name, factor in factors.items():
        out[name] = (out[name] * factor).astype(out[name].dtype)
    return out
```

```python
from contextlib import ExitStack

import numpy as np
import concourse.bass as bass
from concourse import mybir

F32 = mybir.dt.float32
BF16 = mybir.dt.bfloat16
U16 = mybir.dt.uint16
ALU = mybir.AluOpType
ACT = mybir.ActivationFunctionType
AX = mybir.AxisListType

N, C, T = 32, 128, 1024
H, DH, CHUNK = 8, 16, 64
NT = T // 128
K, KP = 30, 32
ROUNDS = KP // 8
EPS = 1e-5
TINY = 1e-20
NEG_BIG = -3.0e38
LAYERS = 3
BPB = 2
BODY = N // BPB
PAIRS = T // (2 * CHUNK)
STEPS = BPB * LAYERS * PAIRS
PASSES = BPB * LAYERS
TILES = BPB * NT
SPAN = STEPS // TILES
HALF = T // 2

LAG_SUM, LAG_T, LAG_PV, LAG_O, LAG_Y = 1, 2, 3, 4, 5
LAG_BN, LAG_LN, LAG_ST = 6, 7, 8
TAIL = LAG_ST
ORDER = range(STEPS + TAIL)


def psum_uses():
    uses = []
    for s in ORDER:
        if s < STEPS and s % (LAYERS * PAIRS) == 0:
            uses += [("xx", s // (LAYERS * PAIRS), h) for h in range(3)]
        if s < STEPS and s % PAIRS == 0:
            uses += [(w, s // PAIRS, h) for w, h in (("q", 0), ("q", 1), ("k", 0), ("k", 1), ("v", 0), ("v", 1))]
        h = s - LAG_O
        if 0 <= h < STEPS and h % 4 == 3:
            uses.append(("y", h // PAIRS, (h % PAIRS) // 4))
    return uses


USES = psum_uses()
USE = {u: n for n, u in enumerate(USES)}
NUSE = len(USES)
assert NUSE % 2 == 0


def flat(ap):
    return ap.rearrange("p a b -> p (a b)")


START = 1


def start_counts(pool, counts):
    for count in counts:
        pool.sem_inc(count, START)


def attention_and_neighbours(nc, dram, keep):
    per_dv = [0]
    with ExitStack() as es:
        def sb(name, shape, dt=F32):
            return es.enter_context(nc.sbuf_tensor(name, shape, dt))

        def ps(name, shape, dt=F32):
            return es.enter_context(nc.psum_tensor(name, shape, dt))

        counts = []

        def sem(name):
            counts.append(es.enter_context(nc.semaphore(name)))
            return counts[-1]

        ident = sb("ident", [128, 128])
        head_mask = sb("head_mask", [128, 8])
        pick3 = sb("pick3", [96, 128], BF16)
        ones3 = sb("ones3", [3, 128], BF16)
        neg3 = sb("neg3", [3, 1])
        half_neg = sb("half_neg", [128, 128])
        w_in = sb("w_in", [128, LAYERS, 3 * C])
        w_out = sb("w_out", [128, LAYERS, C])
        b_in = sb("b_in", [128, LAYERS, 3])
        b_out = sb("b_out", [128, LAYERS])
        pow_half = sb("pow_half", [128, 1])
        perm3 = sb("perm3", [128, 3])
        ctx = sb("ctx", [128, BPB, T])
        xb = sb("xb", [128, BPB, T])
        mask = sb("mask", [128, BPB, T])
        sq = sb("sq", [128, T])
        vrow = sb("vrow", [128, T])
        rest = sb("rest", [128, T])
        dist_row = sb("dist_row", [96, T], BF16)
        mask_row = sb("mask_row", [3, T], BF16)
        xcol = sb("xcol", [128, BPB, 32])
        q_t = sb("q_t", [128, 2, T])
        k_t = sb("k_t", [128, 2, T])
        v_b = sb("v_b", [128, 2, 16, 128])
        q_bd = sb("q_bd", [128, 2, 2, 512])
        prob = sb("prob", [128, 4, 512])
        prob_t = sb("prob_t", [128, 2, 512])
        row_max = sb("row_max", [128, 2, 8])
        row_sum = sb("row_sum", [128, 2, 8])
        row_rec = sb("row_rec", [128, 2, 8])
        o_t = sb("o_t", [128, 2, HALF])
        y_b = sb("y_b", [128, LAYERS, T])
        stats = sb("stats", [128, 2, 6])
        moments = sb("moments", [128, 2, 2])
        rstd = sb("rstd", [128, 2, 3])
        dist = sb("dist", [128, 2, T])
        top8 = sb("top8", [128, ROUNDS, 8])
        nbr = sb("nbr", [128, BPB, NT, KP], U16)

        PJ = ps("PJ", [128, 2, 512])
        PD = ps("PD", [128, 2, 512])
        SC = ps("SC", [128, 2, 512])
        PT = ps("PT", [128, 512])
        OP = ps("OP", [128, 2, 128])

        consts_in = sem("consts_in")
        zeroed = sem("zeroed")
        ctx_in = [sem(f"ctx_in{u}") for u in range(BPB)]
        x_in = [sem(f"x_in{u}") for u in range(BPB)]
        mask_in = [sem(f"mask_in{u}") for u in range(BPB)]
        pj_ready = sem("pj_ready")
        pj_free = [sem(f"pj_free{b}") for b in range(2)]
        squared = sem("squared")
        col_ready = sem("col_ready")
        row_ready = sem("row_ready")
        pool_split = sem("pool_split")
        dist_row_ready = sem("dist_row_ready")
        mask_row_ready = sem("mask_row_ready")
        qbd_ready = sem("qbd_ready")
        scored = sem("scored")
        subbed = sem("subbed")
        exped = sem("exped")
        recip_ready = sem("recip_ready")
        normed = sem("normed")
        transposed = sem("transposed")
        pt_ready = sem("pt_ready")
        pv_ready = sem("pv_ready")
        o_ready = sem("o_ready")
        masked = sem("masked")
        added = sem("added")
        moments_ready = sem("moments_ready")
        pool_ln = sem("pool_ln")
        rstd_ready = sem("rstd_ready")
        applied = [sem(f"applied{j}") for j in range(2)]
        x2_out = [sem(f"x2_out{u}") for u in range(BPB)]
        y3_out = sem("y3_out")
        pd_ready = sem("pd_ready")
        pd_copied = sem("pd_copied")
        topped = sem("topped")
        dve_step = sem("dve_step")
        passed = sem("passed")

        CONSTS = [(ident, dram["ident"]), (head_mask, dram["head_mask"]), (pick3, dram["pick3"]), (ones3, dram["ones3"]),
                  (neg3, dram["neg3"]), (half_neg, dram["half_neg"]), (pow_half, dram["pow_half"]), (perm3, dram["perm3"])]
        NCONST = len(CONSTS) + 4 * LAYERS

        def copied(eng, i, use):
            n = USE[use]
            eng.wait_ge(pj_free[n % 2], START + i * (NUSE // 2) + n // 2 + 1)

        def alone(eng):
            eng.sem_inc(passed, 1)

        block = es.enter_context(nc.Block())

        @block.sync
        def _(sp):
            for tile, src in CONSTS:
                sp.dma_start(tile[:, :], src).then_inc(consts_in, 16)
            for j in range(LAYERS):
                sp.dma_start(w_in[:, j, :], dram["w_in"][j]).then_inc(consts_in, 16)
                sp.dma_start(w_out[:, j, :], dram["w_out"][j]).then_inc(consts_in, 16)
                sp.dma_start(b_in[:, j, :], dram["b_in"][j]).then_inc(consts_in, 16)
                sp.dma_start(b_out[:, j:j + 1], dram["b_out"][j]).then_inc(consts_in, 16)
            with sp.Fori(0, BODY) as i:
                for u in range(BPB):
                    sp.wait_ge(pd_ready, START + i * TILES + NT * (u + 1))
                    sp.dma_start(ctx[:, u, :], dram["ctx"][i * BPB + u]).then_inc(ctx_in[u], 16)
                    sp.wait_ge(masked, START + i * BPB + u + 1)
                    sp.dma_start(mask[:, u, :], dram["mask"][i * BPB + u].broadcast_to([128, T])).then_inc(mask_in[u], 16)
                    sp.wait_ge(x2_out[u], START + i * 16)
                    sp.dma_start(xb[:, u, :], dram["x"][i * BPB + u]).then_inc(x_in[u], 16)


        @block.tensor
        def _(pe):
            pe.sem_inc(pd_ready, TILES)
            pe.wait_ge(consts_in, START + 16 * NCONST)
            pe.wait_ge(zeroed, START + 2)
            with pe.Fori(0, BODY) as i:
                def claim(use):
                    n = USE[use]
                    pe.wait_ge(pj_free[n % 2], START + i * (NUSE // 2) + n // 2)
                    return PJ[:, n % 2, :]

                for s in ORDER:
                    u, w, p = s // (LAYERS * PAIRS), s // PAIRS, s % PAIRS
                    j, c = w % LAYERS, w % 2
                    if s < STEPS and s % (LAYERS * PAIRS) == 0:
                        pe.wait_ge(squared, START + i * BPB + u + 1)
                        for h in range(2):
                            bank = claim(("xx", u, h))
                            pe.matmul(bank, half_neg[:, :], sq[:, h * HALF:(h + 1) * HALF], start=True, stop=True).then_inc(pj_ready, 1)
                        bank = claim(("xx", u, 2))
                        pe.wait_ge(ctx_in[u], START + (i + 1) * 16)
                        for t in range(NT):
                            pe.matmul(bank[:, 8 + 3 * t:11 + 3 * t], ctx[:, u, t * 128:(t + 1) * 128], perm3[:, :], start=True, stop=True)
                        for t in range(NT):
                            last = pe.matmul(bank[:, t:t + 1], sq[:, t * 128:(t + 1) * 128], half_neg[:, 0:1], start=True, stop=True)
                        last.then_inc(pj_ready, 1)
                    if s < STEPS and p == 0:
                        pe.wait_ge(ctx_in[u], START + (i + 1) * 16)
                        for n, name in enumerate("qk"):
                            for h in range(2):
                                bank = claim((name, w, h))
                                pe.matmul(bank, w_in[:, j, n * C:(n + 1) * C], ctx[:, u, h * HALF:(h + 1) * HALF],
                                          start=True, stop=True).then_inc(pj_ready, 1)
                        w_v = w_in[:, j, 2 * C:3 * C].rearrange("p (g e d) -> p e g d", g=4, e=2)
                        for g in range(2):
                            bank = claim(("v", w, g))
                            for m in range(8):
                                t0 = (8 * g + m) * CHUNK
                                for e in range(2):
                                    last = pe.matmul(bank[64 * e:64 * e + 64, m * 64:(m + 1) * 64], ctx[:, u, t0:t0 + CHUNK],
                                                     w_v[:, e, :, :], start=True, stop=True)
                            last.then_inc(pj_ready, 1)
                    if s < STEPS and s % SPAN == 0:
                        tt = s // SPAN
                        t = tt % NT
                        pe.wait_ge(dist_row_ready, START + i * BPB + u + 1)
                        pe.wait_ge(pd_copied, START + i * TILES + tt)
                        for h in range(2):
                            pe.matmul(PD[:, h, :], pick3[:, :], dist_row[:, h * HALF:(h + 1) * HALF], start=True, stop=False)
                            last = pe.matmul(PD[:, h, :], ctx[:, u, t * 128:(t + 1) * 128], ctx[:, u, h * HALF:(h + 1) * HALF],
                                             start=False, stop=True)
                        last.then_inc(pd_ready, 1)
                    if s < STEPS:
                        bank = SC[:, s % 2, :].rearrange("p (c h k) -> p c h k", c=2, h=4)
                        if p == 0:
                            pe.wait_ge(mask_row_ready, START + i * BPB + u + 1)
                            copied(pe, i, ("v", w, 0))
                            copied(pe, i, ("v", w, 1))
                        pe.wait_ge(subbed, START + i * STEPS + max(s - 1, 0))
                        pe.wait_ge(qbd_ready, START + i * STEPS + s + 1)
                        toks = p * 2 * CHUNK
                        rows = mask_row[:, toks:toks + 2 * CHUNK].rearrange("p (c k) -> p c k", c=2).unsqueeze(2).to_broadcast([3, 2, 4, CHUNK])
                        pe.matmul(bank, ones3[:, :], rows, start=True, stop=False, skip_group_check=True)
                        for ch in range(2):
                            for hp in range(4):
                                last = pe.matmul(bank[:, ch, hp, :], q_bd[:, s % 2, ch, hp * 128:(hp + 1) * 128],
                                                 k_t[:, c, toks + ch * CHUNK:toks + (ch + 1) * CHUNK], start=False, stop=True, skip_group_check=True)
                        last.then_inc(scored, 1)
                    r = s - LAG_T
                    if 0 <= r < STEPS:
                        pe.wait_ge(normed, START + i * STEPS + r + 1)
                        pe.wait_ge(pt_ready, START + i * STEPS + r)
                        for m in range(4):
                            last = pe.transpose(PT[:, m * 128:(m + 1) * 128], prob[:, r % 4, m * 128:(m + 1) * 128], ident[:, :])
                        last.then_inc(transposed, 1)
                    r = s - LAG_PV
                    if 0 <= r < STEPS:
                        pe.wait_ge(pt_ready, START + i * STEPS + r + 1)
                        pe.wait_ge(o_ready, START + i * STEPS + r)
                        for ch in range(2):
                            for a in range(2):
                                for b in range(2):
                                    g = 2 * a + b
                                    last = pe.matmul(OP[32 * g:32 * g + 32, r % 2, ch * CHUNK:(ch + 1) * CHUNK],
                                                     v_b[:, (r // PAIRS) % 2, 2 * (r % PAIRS) + ch, 32 * g:32 * g + 32],
                                                     prob_t[:, r % 2, (2 * ch + a) * 128 + b * 64:(2 * ch + a) * 128 + b * 64 + 64],
                                                     start=True, stop=True)
                        last.then_inc(pv_ready, 1)
                    r = s - LAG_O
                    if 0 <= r < STEPS and r % 4 == 3:
                        bank = claim(("y", r // PAIRS, (r % PAIRS) // 4))
                        pe.wait_ge(o_ready, START + i * STEPS + r + 1)
                        pe.matmul(bank, w_out[:, (r // PAIRS) % LAYERS, :], o_t[:, (r // 4) % 2, :], start=True, stop=True).then_inc(pj_ready, 1)

        @block.scalar
        def _(act):
            act.wait_ge(consts_in, START + 16 * NCONST)
            act.wait_ge(zeroed, START + 2)
            with act.Fori(0, BODY) as i:
                def produced(use):
                    n = USE[use]
                    act.wait_ge(pj_ready, START + i * NUSE + n + 1)
                    return PJ[:, n % 2, :], pj_free[n % 2]

                for s in ORDER:
                    u, w, p = s // (LAYERS * PAIRS), s // PAIRS, s % PAIRS
                    j, c = w % LAYERS, w % 2
                    if s < STEPS and s % (LAYERS * PAIRS) == 0:
                        act.wait_ge(ctx_in[u], START + (i + 1) * 16)
                        act.wait_ge(pj_ready, START + (i * NUSE + (USE[("xx", u - 1, 2)] + 1 if u else 0)))
                        act.activation(sq[:, :], ctx[:, u, :], ACT.Square).then_inc(squared, 1)
                        act.wait_ge(dist_row_ready, START + i * BPB + u)
                        for h in range(2):
                            bank, free = produced(("xx", u, h))
                            act.activation(vrow[:, h * HALF:(h + 1) * HALF], bank, ACT.Identity).then_inc(free, 1)
                        bank, free = produced(("xx", u, 2))
                        act.activation(xcol[:, u, :], bank[:, 0:32], ACT.Identity, scale=2.0).then_inc(free, 1)
                        copied(act, i, ("xx", u, 2))
                        act.activation(keep["pts"][:, bass.ds(i * BPB + u, 1), :], xcol[:, u:u + 1, 8:32], ACT.Identity, scale=0.5).then_inc(col_ready, 1)
                    if s < STEPS and p == 0:
                        done = max(PAIRS * (w - 1), 0)
                        act.wait_ge(scored, START + i * STEPS + done)
                        act.wait_ge(qbd_ready, START + i * STEPS + done)
                        for n, (name, dst) in enumerate((("q", q_t), ("k", k_t))):
                            for h in range(2):
                                bank, free = produced((name, w, h))
                                act.activation(dst[:, c, h * HALF:(h + 1) * HALF], bank, ACT.Identity, bias=b_in[:, j, n:n + 1]).then_inc(free, 1)
                        act.wait_ge(pv_ready, START + i * STEPS + done)
                        for g in range(2):
                            bank, free = produced(("v", w, g))
                            for e in range(2):
                                src = bank[64 * e:64 * e + 64, :].rearrange("p (m d) -> p m d", d=DH)
                                dst = v_b[64 * e:64 * e + 64, c, 8 * g:8 * g + 8, :].rearrange("p m (g e d) -> p (m g) e d", g=4, e=2)[:, :, e, :]
                                last = act.activation(dst, src, ACT.Identity)
                            last.then_inc(free, 1)
                    if s < STEPS and s % SPAN == 0:
                        tt = s // SPAN
                        act.wait_ge(pd_ready, START + TILES + i * TILES + tt + 1)
                        act.wait_ge(topped, START + i * TILES + max(tt - 1, 0))
                        act.activation(dist[:, tt % 2, :], flat(PD[:, :, :]), ACT.Identity, scale=2.0,
                                       bias=xcol[:, u, tt % NT:tt % NT + 1]).then_inc(pd_copied, 1)
                    if s < STEPS:
                        act.wait_ge(subbed, START + i * STEPS + s + 1)
                        act.activation(prob[:, s % 4, :], prob[:, s % 4, :], ACT.Exp).then_inc(exped, 1)
                    r = s - LAG_T
                    if 0 <= r < STEPS:
                        act.wait_ge(transposed, START + i * STEPS + r + 1)
                        act.wait_ge(pv_ready, START + i * STEPS + max(r - 1, 0))
                        act.activation(prob_t[:, r % 2, :], PT[:, :], ACT.Identity).then_inc(pt_ready, 1)
                    r = s - LAG_PV
                    if 0 <= r < STEPS:
                        act.wait_ge(pv_ready, START + i * STEPS + r + 1)
                        if r % 4 == 0:
                            before = USE[("y", (r // 4 - 2) // 2, r // 4 % 2)] + 1 if r // 4 >= 2 else 0
                            act.wait_ge(pj_ready, START + i * NUSE + before)
                        act.activation(o_t[:, (r // 4) % 2, (r % 4) * 128:(r % 4 + 1) * 128], OP[:, r % 2, :], ACT.Identity,
                                       bias=b_in[:, (r // PAIRS) % LAYERS, 2:3]).then_inc(o_ready, 1)
                    r = s - LAG_LN
                    if 0 <= r < STEPS and r % PAIRS == PAIRS - 1 and (r // PAIRS) % LAYERS < 2:
                        jj, uu = (r // PAIRS) % LAYERS, r // (LAYERS * PAIRS)
                        act.wait_ge(rstd_ready, START + i * 2 * BPB + 2 * uu + jj + 1)
                        act.activation(xb[:, uu, :], y_b[:, jj, :], ACT.Identity, scale=rstd[:, jj, 1:2], bias=rstd[:, jj, 2:3]).then_inc(applied[jj], 1)
                    r = s - LAG_ST
                    if 0 <= r < STEPS and r % PAIRS == PAIRS - 1:
                        jj, uu = (r // PAIRS) % LAYERS, r // (LAYERS * PAIRS)
                        if jj == 1:
                            act.wait_ge(applied[1], START + i * BPB + uu + 1)
                            act.dma_start(dram["x2"][i * BPB + uu], xb[:, uu, :]).then_inc(x2_out[uu], 16)
                        if jj == 2:
                            act.wait_ge(masked, START + BPB + i * BPB + uu + 1)
                            act.dma_start(dram["y3"][i * BPB + uu], y_b[:, 2, :]).then_inc(y3_out, 16)
            for u in range(BPB):
                act.wait_ge(x2_out[u], START + BODY * 16)
            act.wait_ge(y3_out, START + N * 16)

        @block.gpsimd
        def _(pool):
            start_counts(pool, counts)
            pool.memset(v_b[:, 0, :, :], 0.0).then_inc(zeroed, 1)
            pool.memset(v_b[:, 1, :, :], 0.0).then_inc(zeroed, 1)
            pool.wait_ge(consts_in, START + 16 * NCONST)
            with pool.Fori(0, BODY) as i:
                split = 0
                lnstep = 0
                for s in ORDER:
                    u, w, p = s // (LAYERS * PAIRS), s // PAIRS, s % PAIRS
                    c = w % 2
                    if s < STEPS and s % (LAYERS * PAIRS) == 0:
                        pool.wait_ge(col_ready, START + i * BPB + u + 1)
                        pool.wait_ge(pd_ready, START + TILES + i * TILES + NT * u)
                        pool.wait_ge(normed, START + i * STEPS + max(s - LAG_SUM, 0))
                        pool.wait_ge(qbd_ready, START + i * STEPS + s)
                        pool.wait_ge(rstd_ready, START + i * 2 * BPB + 2 * u)
                        pool.wait_ge(added, START + i * 4 * BPB + 4 * u)
                        alone(pool)
                        def then(ins):
                            nonlocal split
                            split += 1
                            ins.then_inc(pool_split, 1)
                            pool.wait_ge(pool_split, START + i * SPLITS + split)
                            alone(pool)

                        then(pool.tensor_copy(dist_row[0:96, :], vrow[0:96, :]))
                        then(pool.tensor_tensor(rest[0:96, :], vrow[0:96, :], dist_row[0:96, :], ALU.subtract))
                        then(pool.tensor_copy(dist_row[32:64, :], rest[32:64, :]))
                        then(pool.tensor_copy(dist_row[64:96, :], rest[64:96, :]))
                        then(pool.tensor_tensor(rest[64:96, :], rest[64:96, :], dist_row[64:96, :], ALU.subtract))
                        pool.tensor_copy(dist_row[64:96, :], rest[64:96, :]).then_inc(dist_row_ready, 1)
                        pool.wait_ge(dist_row_ready, START + i * BPB + u + 1)
                    if s < STEPS:
                        if p == 0:
                            copied(pool, i, ("q", w, 0))
                            copied(pool, i, ("q", w, 1))
                        pool.wait_ge(scored, START + i * STEPS + max(s - 1, 0))
                        for ch in range(2):
                            t0 = (2 * p + ch) * CHUNK
                            qq = q_t[:, c, t0:t0 + CHUNK].unsqueeze(1).to_broadcast([128, 8, CHUNK])
                            hm = head_mask[:, :].unsqueeze(2).to_broadcast([128, 8, CHUNK])
                            last = pool.tensor_tensor(q_bd[:, s % 2, ch, :].rearrange("p (h k) -> p h k", h=8), qq, hm, ALU.mult)
                        last.then_inc(qbd_ready, 1)
                    r = s - LAG_SUM
                    if 0 <= r < STEPS:
                        pool.wait_ge(recip_ready, START + i * STEPS + r + 1)
                        pr = prob[:, r % 4, :].rearrange("p (h k) -> p h k", h=8)
                        pool.tensor_tensor(pr, pr, row_rec[:, r % 2, :].unsqueeze(2).to_broadcast([128, 8, CHUNK]), ALU.mult).then_inc(normed, 1)
                    r = s - LAG_Y
                    if 0 <= r < STEPS and r % 4 == 3 and (r // PAIRS) % LAYERS < 2:
                        jj, uu, h = (r // PAIRS) % LAYERS, r // (LAYERS * PAIRS), (r % PAIRS) // 4
                        copied(pool, i, ("y", r // PAIRS, h))
                        if jj == 0:
                            pool.wait_ge(x_in[uu], START + (i + 1) * 16)
                        else:
                            pool.wait_ge(applied[0], START + i * BPB + uu + 1)
                        half = slice(h * HALF, (h + 1) * HALF)
                        pool.tensor_tensor(y_b[:, jj, half], y_b[:, jj, half], xb[:, uu, half], ALU.add).then_inc(added, 1)
                    r = s - LAG_BN
                    if 0 <= r < STEPS and r % PAIRS == PAIRS - 1 and (r // PAIRS) % LAYERS < 2:
                        jj, uu = (r // PAIRS) % LAYERS, r // (LAYERS * PAIRS)
                        pool.wait_ge(moments_ready, START + i * 2 * BPB + 2 * uu + jj + 1)
                        pool.wait_ge(applied[jj], START + i * BPB + uu)
                        alone(pool)
                        pool.tensor_scalar(rstd[:, jj, 0:1], moments[:, jj, 1:2], 1.0, EPS, ALU.mult, ALU.add).then_inc(pool_ln, 1)
                        pool.wait_ge(pool_ln, START + i * 4 * BPB + lnstep + 1)
                        pool.tensor_tensor(rstd[:, jj, 1:2], rstd[:, jj, 0:1], pow_half[:, :], ALU.pow).then_inc(pool_ln, 1)
                        pool.wait_ge(pool_ln, START + i * 4 * BPB + lnstep + 2)
                        alone(pool)
                        pool.tensor_scalar(rstd[:, jj, 2:3], moments[:, jj, 0:1], rstd[:, jj, 1:2], -1.0, ALU.mult, ALU.mult).then_inc(rstd_ready, 1)
                        lnstep += 2
                assert split == SPLITS and lnstep == 4 * BPB

        @block.vector
        def _(dve):
            dve.sem_inc(masked, BPB)
            dve.wait_ge(consts_in, START + 16 * NCONST)
            with dve.Fori(0, BODY) as i:
                def link(ins, plain=False):
                    per_dv[0] += 1
                    ins.then_inc(dve_step, 1)
                    dve.wait_ge(dve_step, START + i * DVE_STEPS + per_dv[0])
                    if plain:
                        alone(dve)

                for s in ORDER:
                    u, w, p = s // (LAYERS * PAIRS), s // PAIRS, s % PAIRS
                    if s < STEPS and s % (LAYERS * PAIRS) == 0:
                        dve.wait_ge(mask_in[u], START + (i + 1) * 16)
                        dve.wait_ge(scored, START + i * STEPS + s)
                        dve.tensor_scalar(mask_row[:, :], mask[0:3, u, :], 0.0, neg3[:, 0:1], ALU.is_le, ALU.mult).then_inc(mask_row_ready, 1)
                    r = s - LAG_Y
                    if 0 <= r < STEPS and r % 4 == 3:
                        ww, jj, uu, h = r // PAIRS, (r // PAIRS) % LAYERS, r // (LAYERS * PAIRS), (r % PAIRS) // 4
                        n = USE[("y", ww, h)]
                        dve.wait_ge(pj_ready, START + i * NUSE + n + 1)
                        if h == 0:
                            if jj < 2:
                                dve.wait_ge(applied[jj], START + i * BPB + uu)
                            else:
                                dve.wait_ge(y3_out, START + (i * BPB + uu) * 16)
                        half = slice(h * HALF, (h + 1) * HALF)
                        dve.scalar_tensor_tensor(y_b[:, jj, half], PJ[:, n % 2, :], b_out[:, jj:jj + 1], mask[:, uu, half],
                                                 ALU.add, ALU.mult).then_inc(pj_free[n % 2], 1)
                        if jj == LAYERS - 1 and h == 1:
                            copied(dve, i, ("y", ww, 0))
                            copied(dve, i, ("y", ww, 1))
                            dve.sem_inc(masked, 1)
                    if s < STEPS:
                        dve.wait_ge(scored, START + i * STEPS + s + 1)
                        dve.wait_ge(transposed, START + i * STEPS + max(s - 3, 0))
                        bank = SC[:, s % 2, :].rearrange("p (h k) -> p h k", h=8)
                        link(dve.tensor_reduce(row_max[:, s % 2, :], bank, AX.X, ALU.max))
                        dve.tensor_tensor(prob[:, s % 4, :].rearrange("p (h k) -> p h k", h=8), bank,
                                          row_max[:, s % 2, :].unsqueeze(2).to_broadcast([128, 8, CHUNK]), ALU.subtract).then_inc(subbed, 1)
                    r = s - LAG_SUM
                    if 0 <= r < STEPS:
                        dve.wait_ge(exped, START + i * STEPS + r + 1)
                        link(dve.tensor_reduce(row_sum[:, r % 2, :], prob[:, r % 4, :].rearrange("p (h k) -> p h k", h=8), AX.X, ALU.add))
                        dve.wait_ge(normed, START + i * STEPS + max(r - 1, 0))
                        dve.reciprocal(row_rec[:, r % 2, :], row_sum[:, r % 2, :]).then_inc(recip_ready, 1)
                    r = s - LAG_BN
                    if 0 <= r < STEPS and r % PAIRS == PAIRS - 1 and (r // PAIRS) % LAYERS < 2:
                        jj, uu = (r // PAIRS) % LAYERS, r // (LAYERS * PAIRS)
                        dve.wait_ge(added, START + i * 4 * BPB + 4 * uu + 2 * jj + 2)
                        dve.bn_stats(stats[:, 0, :], y_b[:, jj, 0:HALF])
                        link(dve.bn_stats(stats[:, 1, :], y_b[:, jj, HALF:T]), plain=True)
                        dve.bn_aggr(moments[:, jj, :], stats[:, :, :]).then_inc(moments_ready, 1)
                    if s < STEPS and s % SPAN == 1:
                        tt = s // SPAN
                        t = tt % NT
                        dve.wait_ge(pd_copied, START + i * TILES + tt + 1)
                        alone(dve)
                        for k in range(ROUNDS):
                            link(dve.max(top8[:, k, :], dist[:, tt % 2, :]), plain=True)
                            if k < ROUNDS - 1:
                                dve.max_index(nbr[:, u, t, k * 8:(k + 1) * 8], top8[:, k, :], dist[:, tt % 2, :])
                                link(dve.match_replace(dist[:, tt % 2, :], top8[:, k, :], dist[:, tt % 2, :], NEG_BIG), plain=True)
                            else:
                                dve.max_index(nbr[:, u, t, k * 8:(k + 1) * 8], top8[:, k, :], dist[:, tt % 2, :]).then_inc(topped, 1)
                        if t == NT - 1:
                            dve.wait_ge(topped, START + i * TILES + tt + 1)
                            link(dve.tensor_copy(keep["nbr"][:, bass.ds(i * BPB + u, 1), :],
                                            nbr[:, u:u + 1, :, :].rearrange("p u t k -> p u (t k)")))
                assert per_dv[0] == DVE_STEPS, per_dv[0]



SPLITS = 5 * BPB
DVE_STEPS = 2 * STEPS + TILES * (2 * ROUNDS - 1) + BPB + 2 * BPB


KQ = 4
QUADS = -(-K // KQ)
SPLIT_K = 21
NF = NT * K


def spherical_features(nc, dram, keep):
    with ExitStack() as es:
        def sb(name, shape, dt=F32):
            return es.enter_context(nc.sbuf_tensor(name, shape, dt))

        def ps(name, shape, dt=F32):
            return es.enter_context(nc.psum_tensor(name, shape, dt))

        counts = []

        def sem(name):
            counts.append(es.enter_context(nc.semaphore(name)))
            return counts[-1]

        ident_b = sb("ident_b", [128, 128], BF16)
        pick_k = sb("pick_k", [98, K, 128], BF16)
        iota8 = sb("iota8", [128, 8])
        low_u = sb("low_u", [128, NT * KP], U16)
        high_u = sb("high_u", [128, NT * KP], U16)
        low = sb("low", [128, NT * KP], BF16)
        high = sb("high", [128, NT * KP])
        oh_b = sb("oh_b", [128, NT * KP, 8])
        rows = sb("rows", [98, T], BF16)
        low2 = sb("low2", [32, T])
        low2_b = sb("low2_b", [32, T], BF16)
        own = sb("own", [128, NT, 3])
        table = sb("table", [128, 3, 24], BF16)
        left = sb("left", [128, 2, 24])
        oh_a = sb("oh_a", [128, 2, 512], BF16)
        cand = sb("cand", [128, 2, K * 24])
        rel = sb("rel", [128, 3, NT, K])
        sqr = sb("sqr", [128, 3, NF])
        r2 = sb("r2", [128, 2, NF])
        r2m = sb("r2m", [128, 2, NF])
        root = sb("root", [128, 2, NF])
        good = sb("good", [128, 2, NF])
        degen = sb("degen", [128, 2, NF])
        yy = sb("yy", [128, 2, NF])
        xx = sb("xx", [128, 2, NF])
        ay = sb("ay", [128, 2, NF])
        ax = sb("ax", [128, 2, NF])
        big = sb("big", [128, 2, NF])
        ratio = sb("ratio", [128, 2, NF])
        at = sb("at", [128, 2, NF])
        flag = sb("flag", [128, 2, NF])
        turn = sb("turn", [128, 2, NF])

        BC = ps("BC", [128, 2, 512])
        LT = ps("LT", [32, T], BF16)
        G = ps("G", [128, 2, 2, 512])

        consts_in = sem("b_consts_in")
        low_ready = sem("low_ready")
        lt_ready = sem("lt_ready")
        lt_copied = sem("lt_copied")
        rows_ready = sem("rows_ready")
        own_ready = sem("own_ready")
        table_step = sem("table_step")
        table_ready = sem("table_ready")
        bc_ready = sem("bc_ready")
        oh_ready = sem("oh_ready")
        fetched = sem("fetched")
        g_free = sem("g_free")
        r2_ready = sem("r2_ready")
        root_ready = sem("root_ready")
        yx_ready = sem("yx_ready")
        abs_ready = sem("abs_ready")
        ratio_ready = sem("ratio_ready")
        at_ready = sem("at_ready")
        dstep = sem("b_dstep")
        passed = sem("b_passed")
        NCONST = 3

        block = es.enter_context(nc.Block())

        @block.sync
        def _(sp):
            sp.dma_start(ident_b[:, :], dram["ident_b"]).then_inc(consts_in, 16)
            sp.dma_start(pick_k[:, :, :], dram["pick_k"]).then_inc(consts_in, 16)
            sp.dma_start(iota8[:, :], dram["iota8"]).then_inc(consts_in, 16)
            sp.wait_ge(consts_in, START + 16 * NCONST)

        @block.gpsimd
        def _(pool):
            start_counts(pool, counts)
            with pool.Fori(0, N) as i:
                n = 0

                def then(ins):
                    nonlocal n
                    n += 1
                    ins.then_inc(table_step, 1)
                    pool.wait_ge(table_step, START + i * 4 + n)
                    pool.sem_inc(passed, 1)

                pool.wait_ge(own_ready, START + i + 1)
                pool.wait_ge(fetched, START + i * NT * QUADS)
                pool.sem_inc(passed, 1)
                src = own[:, :, :].rearrange("p t c -> p (t c)")
                then(pool.tensor_copy(table[:, 0, :], src))
                then(pool.tensor_tensor(left[:, 0, :], src, table[:, 0, :], ALU.subtract))
                then(pool.tensor_copy(table[:, 1, :], left[:, 0, :]))
                then(pool.tensor_tensor(left[:, 1, :], left[:, 0, :], table[:, 1, :], ALU.subtract))
                pool.tensor_copy(table[:, 2, :], left[:, 1, :]).then_inc(table_ready, 1)

        @block.tensor
        def _(pe):
            pe.wait_ge(consts_in, START + 16 * NCONST)
            with pe.Fori(0, N) as i:
                pe.wait_ge(low_ready, START + i + 1)
                pe.wait_ge(rows_ready, START + i)
                for t in range(NT):
                    last = pe.transpose(LT[:, t * 128:(t + 1) * 128], low[:, t * KP:(t + 1) * KP], ident_b[:, :])
                last.then_inc(lt_ready, 1)
                pe.wait_ge(rows_ready, START + i + 1)
                pe.wait_ge(table_ready, START + i + 1)
                for x in range(NT * QUADS + 1):
                    if x < NT * QUADS:
                        t, q = x // QUADS, x % QUADS
                        pe.wait_ge(oh_ready, START + i * NT * QUADS + max(x - 1, 0))
                        for k in range(q * KQ, min(q * KQ + KQ, K)):
                            last = pe.matmul(BC[:, x % 2, (k % KQ) * 128:(k % KQ + 1) * 128], pick_k[:, k, :],
                                             rows[:, t * 128:(t + 1) * 128], start=True, stop=True)
                        last.then_inc(bc_ready, 1)
                    x -= 1
                    if x >= 0:
                        t, q = x // QUADS, x % QUADS
                        if q == 0:
                            pe.wait_ge(g_free, START + i * NT + max(t - 1, 0))
                        pe.wait_ge(oh_ready, START + i * NT * QUADS + x + 1)
                        for k in range(q * KQ, min(q * KQ + KQ, K)):
                            half, at_k = (0, k) if k < SPLIT_K else (1, k - SPLIT_K)
                            for part in range(3):
                                last = pe.matmul(G[:, t % 2, half, at_k * 24:at_k * 24 + 24], oh_a[:, x % 2, (k % KQ) * 128:(k % KQ + 1) * 128],
                                                 table[:, part, :], start=(part == 0), stop=(part == 2))
                        last.then_inc(fetched, 1)

        @block.scalar
        def _(act):
            with act.Fori(0, N) as i:
                act.wait_ge(rows_ready, START + i)
                act.wait_ge(lt_ready, START + i + 1)
                act.activation(low2[:, :], LT[:, :], ACT.Square)
                act.activation(rows[0:32, :], LT[:, :], ACT.Identity).then_inc(lt_copied, 1)
                for x in range(NT * QUADS):
                    cols = (min(KQ, K - (x % QUADS) * KQ)) * 128
                    act.wait_ge(bc_ready, START + i * NT * QUADS + x + 1)
                    act.wait_ge(fetched, START + i * NT * QUADS + max(x - 1, 0))
                    act.activation(oh_a[:, x % 2, 0:cols], BC[:, x % 2, 0:cols], ACT.Relu, scale=-1.0, bias=1.0).then_inc(oh_ready, 1)
                act.wait_ge(r2_ready, START + i + 1)
                act.activation(root[:, :, :], r2m[:, :, :], ACT.Sqrt).then_inc(root_ready, 1)
                act.wait_ge(root_ready, START + i + 1)
                act.activation(keep["sph"][:, 0:1, bass.ds(i, 1), :], root[:, 0:1, :].unsqueeze(2), ACT.Identity)
                act.wait_ge(yx_ready, START + i + 1)
                act.activation(ay[:, :, :], yy[:, :, :], ACT.Abs)
                act.activation(ax[:, :, :], xx[:, :, :], ACT.Abs).then_inc(abs_ready, 1)
                act.wait_ge(ratio_ready, START + i + 1)
                act.activation(at[:, :, :], ratio[:, :, :], ACT.Arctan).then_inc(at_ready, 1)

        @block.vector
        def _(dve):
            dve.memset(rows[96:98, :], 1.0)
            dve.wait_ge(consts_in, START + 16 * NCONST)
            with dve.Fori(0, N) as i:
                n = 0

                def link(ins):
                    nonlocal n
                    n += 1
                    ins.then_inc(dstep, 1)
                    dve.wait_ge(dstep, START + i * B_STEPS + n)

                dve.wait_ge(lt_ready, START + i)
                here = keep["nbr"][:, bass.ds(i, 1), :].rearrange("p u k -> p (u k)")
                link(dve.tensor_copy(high_u[:, :], here))
                link(dve.tensor_scalar(low_u[:, :], high_u[:, :], 127, None, ALU.bitwise_and))
                dve.tensor_copy(low[:, :], low_u[:, :]).then_inc(low_ready, 1)
                link(dve.tensor_scalar(high_u[:, :], high_u[:, :], 7, None, ALU.logical_shift_right))
                link(dve.tensor_copy(high[:, :], high_u[:, :]))
                dve.wait_ge(table_ready, START + i)
                dve.tensor_copy(own[:, :, :].rearrange("p t c -> p (t c)"), keep["pts"][:, bass.ds(i, 1), :].rearrange("p u k -> p (u k)")).then_inc(own_ready, 1)
                link(dve.tensor_tensor(oh_b[:, :, :], high[:, :].unsqueeze(2).to_broadcast([128, NT * KP, 8]),
                                       iota8[:, :].unsqueeze(1).to_broadcast([128, NT * KP, 8]), ALU.is_equal))
                dve.wait_ge(lt_copied, START + i + 1)
                link(dve.tensor_copy(low2_b[:, :], low2[:, :]))
                dve.tensor_copy(rows[32:64, :], low2_b[:, :])
                link(dve.tensor_tensor(rows[64:96, :], low2[:, :], low2_b[:, :], ALU.subtract))
                dve.sem_inc(rows_ready, 1)
                for t in range(NT):
                    dve.wait_ge(fetched, START + (i * NT + t + 1) * QUADS)
                    for half, k0, k1 in ((0, 0, SPLIT_K), (1, SPLIT_K, K)):
                        src = G[:, t % 2, half, 0:(k1 - k0) * 24].rearrange("p (k b c) -> p k b c", b=8, c=3)
                        dst = cand[:, t % 2, k0 * 24:k1 * 24].rearrange("p (k b c) -> p k b c", b=8, c=3)
                        ohs = oh_b[:, t * KP + k0:t * KP + k1, :].unsqueeze(3).to_broadcast([128, k1 - k0, 8, 3])
                        last = dve.tensor_tensor(dst, src, ohs, ALU.mult)
                    last.then_inc(g_free, 1)
                    dve.wait_ge(g_free, START + i * NT + t + 1)
                    last = dve.tensor_reduce(rel[:, :, t, :].rearrange("p c k -> p k c"),
                                             cand[:, t % 2, :].rearrange("p (k b c) -> p k c b", b=8, c=3), AX.X, ALU.add)
                link(last)
                link(dve.tensor_tensor(rel[:, :, :, :], rel[:, :, :, :],
                                       own[:, :, :].rearrange("p t c -> p c t").unsqueeze(3).to_broadcast([128, 3, NT, K]), ALU.subtract))
                rl = rel[:, :, :, :].rearrange("p c t k -> p c (t k)")
                link(dve.tensor_tensor(sqr[:, :, :], rl, rl, ALU.mult))
                link(dve.tensor_tensor(r2[:, 1, :], sqr[:, 0, :], sqr[:, 2, :], ALU.add))
                link(dve.tensor_tensor(r2[:, 0, :], r2[:, 1, :], sqr[:, 1, :], ALU.add))
                dve.tensor_scalar(r2m[:, :, :], r2[:, :, :], TINY, None, ALU.max).then_inc(r2_ready, 1)
                link(dve.tensor_scalar(good[:, :, :], r2[:, :, :], TINY, None, ALU.is_ge))
                link(dve.tensor_scalar(degen[:, :, :], r2[:, :, :], TINY, None, ALU.is_lt))
                dve.tensor_tensor(yy[:, :, :], rl[:, 1:3, :], good[:, :, :], ALU.mult)
                dve.wait_ge(root_ready, START + i + 1)
                link(dve.tensor_tensor(xx[:, 0, :], root[:, 1, :], good[:, 0, :], ALU.mult))
                link(dve.tensor_tensor(xx[:, 1, :], rl[:, 0, :], good[:, 1, :], ALU.mult))
                dve.tensor_tensor(xx[:, :, :], xx[:, :, :], degen[:, :, :], ALU.add).then_inc(yx_ready, 1)
                dve.wait_ge(abs_ready, START + i + 1)
                link(dve.tensor_tensor(big[:, :, :], ax[:, :, :], ay[:, :, :], ALU.max))
                link(dve.reciprocal(big[:, :, :], big[:, :, :]))
                link(dve.tensor_tensor(ratio[:, :, :], ax[:, :, :], ay[:, :, :], ALU.min))
                dve.tensor_tensor(ratio[:, :, :], ratio[:, :, :], big[:, :, :], ALU.mult).then_inc(ratio_ready, 1)
                link(dve.tensor_tensor(flag[:, :, :], ay[:, :, :], ax[:, :, :], ALU.is_gt))
                link(dve.tensor_scalar(turn[:, :, :], flag[:, :, :], -2.0, 1.0, ALU.mult, ALU.add))
                dve.wait_ge(at_ready, START + i + 1)
                link(dve.tensor_tensor(at[:, :, :], at[:, :, :], turn[:, :, :], ALU.mult))
                link(dve.scalar_tensor_tensor(at[:, :, :], flag[:, :, :], float(np.pi / 2), at[:, :, :], ALU.mult, ALU.add))
                link(dve.tensor_scalar(flag[:, :, :], xx[:, :, :], 0.0, None, ALU.is_lt))
                link(dve.tensor_scalar(turn[:, :, :], flag[:, :, :], -2.0, 1.0, ALU.mult, ALU.add))
                link(dve.tensor_tensor(at[:, :, :], at[:, :, :], turn[:, :, :], ALU.mult))
                link(dve.scalar_tensor_tensor(at[:, :, :], flag[:, :, :], float(np.pi), at[:, :, :], ALU.mult, ALU.add))
                link(dve.tensor_scalar(flag[:, :, :], yy[:, :, :], 0.0, None, ALU.is_lt))
                link(dve.tensor_scalar(turn[:, :, :], flag[:, :, :], -2.0, 1.0, ALU.mult, ALU.add))
                link(dve.tensor_tensor(keep["sph"][:, 1:3, bass.ds(i, 1), :], at[:, :, :].unsqueeze(2), turn[:, :, :].unsqueeze(2), ALU.mult))
                assert n == B_STEPS, n


B_STEPS = 30


M_ALL = float(N * T * K)
COLS = N * NF
PIECES = 8
PIECE = COLS // PIECES
SLOPE = 0.2
SERIAL = ["sum1", "all1", "centred", "squares1", "sum_sq1", "all_sq1", "var1", "pow1", "u1",
          "sum2", "all2", "mean2", "squares2", "sum_sq2", "all_sq2", "var2", "pow2", "shift2",
          "sum3", "all3", "mean3", "squares3", "sum_sq3", "all_sq3", "var3", "pow3", "shift3",
          "logit", "less_top", "exp"]


def batch_norms(nc, dram, keep):
    S = keep["sph"][:, :, :, :].rearrange("p c n k -> p c (n k)")
    att = keep["sph"][:, :, :, :].rearrange("p c n k -> p (c n k)")[:, COLS:COLS + N * NT * KP].rearrange("p (m k) -> p m k", k=KP)
    with ExitStack() as es:
        def sb(name, shape, dt=F32):
            return es.enter_context(nc.sbuf_tensor(name, shape, dt))

        def ps(name, shape, dt=F32):
            return es.enter_context(nc.psum_tensor(name, shape, dt))

        def sem(name):
            return es.enter_context(nc.semaphore(name))

        w1 = sb("w1", [128, 6, 6])
        w2 = sb("w2", [128, 3, 6])
        w3 = sb("w3", [128, 3])
        gains = [sb(f"g{n}", [128, w]) for n, w in ((1, 6), (2, 3), (3, 1))]
        shifts = [sb(f"b{n}", [128, w]) for n, w in ((1, 6), (2, 3), (3, 1))]
        ones = sb("c_ones", [128, 128])
        minus_half = sb("minus_half", [128, 6])
        part = sb("part", [128, 6, PIECES])
        partial = sb("partial", [128, 6])
        mean = sb("mean", [128, 3])
        neg_mean = sb("neg_mean", [128, 3])
        cov = sb("cov", [128, 9])
        w1s = sb("w1s", [128, 6])
        v1 = sb("v1", [128, 6, 3])
        vc = sb("vc", [128, 6, 3, 3])
        var = sb("var", [128, 6])
        var_eps = sb("var_eps", [128, 6])
        inv = sb("inv", [128, 6])
        gain = sb("gain", [128, 6])
        shift = sb("shift", [128, 6])
        u1 = sb("u1", [128, 6, 3])
        junk = sb("junk", [128, PIECE])
        junk_a = sb("junk_a", [128, PIECE])
        u = sb("u", [128, 2, PIECE])
        h = sb("h", [128, 2, PIECE])
        p2 = sb("p2", [128, 3, PIECE])
        top = sb("top", [128, N * NT])
        total = sb("total", [128, N * NT])
        SUM = ps("SUM", [128, 16])

        par_in = sem("par_in")
        serial = sem("serial")
        lin = sem("lin")
        lrelued = sem("lrelued")
        used_h = sem("used_h")
        act_g = sem("act_g")
        used_g = sem("used_g")
        dlink = sem("c_dlink")
        plink = sem("c_plink")
        alink = sem("c_alink")
        block = es.enter_context(nc.Block())

        def wait(eng, name):
            eng.wait_ge(serial, SERIAL.index(name) + 1)

        def mark(ins):
            ins.then_inc(serial, 1)

        def piece(x):
            return slice(x * PIECE, (x + 1) * PIECE)

        small = [(w1[:, :, :].rearrange("p a b -> p (a b)"), "W1"), (w2[:, :, :].rearrange("p a b -> p (a b)"), "W2"), (w3[:, :], "W3")]
        small += [(gains[n][:, :], f"g{n + 1}") for n in range(3)] + [(shifts[n][:, :], f"b{n + 1}") for n in range(3)]

        @block.sync
        def _(sp):
            for dst, name in small:
                sp.dma_start(dst, dram[name].broadcast_to([128, dst.shape[1]])).then_inc(par_in, 16)
            sp.wait_ge(par_in, 16 * len(small))

        @block.tensor
        def _(pe):
            for before, name, cols in (("sum1", "all1", 3), ("sum_sq1", "all_sq1", 6), ("sum2", "all2", 3), ("sum_sq2", "all_sq2", 3),
                                       ("sum3", "all3", 1), ("sum_sq3", "all_sq3", 1)):
                wait(pe, before)
                mark(pe.matmul(SUM[:, 0:cols], ones[:, :], partial[:, 0:cols], start=True, stop=True))

        @block.gpsimd
        def _(pool):
            pool.memset(minus_half[:, :], -0.5).then_inc(plink, 1)
            pool.wait_ge(plink, 1)
            n = 1
            for name in ("1", "2", "3"):
                wait(pool, "var" + name)
                pool.tensor_scalar(var_eps[:, :], var[:, :], 1.0, EPS, ALU.mult, ALU.add).then_inc(plink, 1)
                n += 1
                pool.wait_ge(plink, n)
                mark(pool.tensor_tensor(inv[:, :], var_eps[:, :], minus_half[:, :], ALU.pow))

        @block.scalar
        def _(act):
            n = 0

            def squares(width, centre=False):
                nonlocal n
                for c in range(width):
                    for x in range(PIECES):
                        mean_c = {"bias": neg_mean[:, c:c + 1]} if centre else {}
                        last = act.activation(junk_a[:, :], S[:, c, piece(x)], ACT.Square, accum_out=part[:, c, x:x + 1], **mean_c)
                        if (c, x) == (width - 1, PIECES - 1):
                            mark(last)
                        else:
                            n += 1
                            last.then_inc(alink, 1)
                            act.wait_ge(alink, n)

            act.wait_ge(par_in, 16 * len(small))
            wait(act, "centred")
            squares(3)
            wait(act, "u1")
            for y in range(6 * PIECES):
                x, j = y // 6, y % 6
                act.wait_ge(lrelued, max(y - 1, 0))
                act.activation(u[:, y % 2, :], S[:, 0, piece(x)], ACT.Identity, scale=u1[:, j, 0:1], bias=shifts[0][:, j:j + 1]).then_inc(lin, 1)
            wait(act, "mean2")
            squares(3, centre=True)
            wait(act, "shift2")
            for y in range(3 * PIECES):
                x, o = y // 3, y % 3
                act.wait_ge(lrelued, 6 * PIECES + max(y - 1, 0))
                act.activation(u[:, y % 2, :], S[:, o, piece(x)], ACT.Identity, scale=gain[:, o:o + 1], bias=shift[:, o:o + 1]).then_inc(act_g, 1)
            wait(act, "mean3")
            squares(1, centre=True)
            wait(act, "shift3")
            mark(act.activation(S[:, 0, :], S[:, 0, :], ACT.Identity, scale=gain[:, 0:1], bias=shift[:, 0:1]))
            wait(act, "less_top")
            mark(act.activation(S[:, 0, :], S[:, 0, :], ACT.Exp))

        @block.vector
        def _(dve):
            n = 0

            def link(ins):
                nonlocal n
                n += 1
                ins.then_inc(dlink, 1)
                dve.wait_ge(dlink, n)

            link(dve.memset(ones[:, :], 1.0))
            link(dve.memset(var[:, :], 1.0))
            dve.wait_ge(par_in, 16 * len(small))
            link(dve.tensor_reduce(w1s[:, :], w1[:, :, 3:6], AX.X, ALU.add))
            link(dve.tensor_tensor(v1[:, :, :], w1[:, :, 0:3], w1[:, :, 3:6], ALU.add))
            link(dve.scalar_tensor_tensor(v1[:, :, :], w1s[:, :].unsqueeze(2).to_broadcast([128, 6, 3]), -1.0 / 3.0, v1[:, :, :], ALU.mult, ALU.add))
            mark(dve.tensor_reduce(partial[:, 0:3], S, AX.X, ALU.add))
            wait(dve, "all1")
            link(dve.tensor_scalar(mean[:, :], SUM[:, 0:3], 1.0 / M_ALL, None, ALU.mult))
            for c in range(3):
                last = dve.tensor_scalar(S[:, c, :], S[:, c, :], mean[:, c:c + 1], None, ALU.subtract)
            mark(last)
            wait(dve, "centred")
            for m, (a, b) in enumerate(((0, 1), (0, 2), (1, 2))):
                for x in range(PIECES):
                    link(dve.tensor_tensor_reduce(junk[:, :], S[:, a, piece(x)], S[:, b, piece(x)], 1.0, 0.0, ALU.mult, ALU.add,
                                                  part[:, 3 + m, x:x + 1]))
            wait(dve, "squares1")
            mark(dve.tensor_reduce(partial[:, :], part[:, :, :], AX.X, ALU.add))
            wait(dve, "all_sq1")
            scale = 1.0 / M_ALL
            dve.tensor_scalar(cov[:, 0:9:4], SUM[:, 0:3], scale, None, ALU.mult)
            dve.tensor_scalar(cov[:, 1:3], SUM[:, 3:5], scale, None, ALU.mult)
            dve.tensor_scalar(cov[:, 3:7:3], SUM[:, 3:5], scale, None, ALU.mult)
            dve.tensor_scalar(cov[:, 5:6], SUM[:, 5:6], scale, None, ALU.mult)
            link(dve.tensor_scalar(cov[:, 7:8], SUM[:, 5:6], scale, None, ALU.mult))
            full = [128, 6, 3, 3]
            link(dve.tensor_tensor(vc[:, :, :, :], v1[:, :, :].unsqueeze(3).to_broadcast(full),
                                   cov[:, :].rearrange("p (a b) -> p a b", a=3).unsqueeze(1).to_broadcast(full), ALU.mult))
            link(dve.tensor_tensor(vc[:, :, :, :], vc[:, :, :, :], v1[:, :, :].unsqueeze(2).to_broadcast(full), ALU.mult))
            mark(dve.tensor_reduce(var[:, :], vc[:, :, :, :].rearrange("p j a b -> p j (a b)"), AX.X, ALU.add))
            wait(dve, "pow1")
            link(dve.tensor_tensor(gain[:, :], inv[:, :], gains[0][:, :], ALU.mult))
            mark(dve.tensor_tensor(u1[:, :, :], v1[:, :, :], gain[:, :].unsqueeze(2).to_broadcast([128, 6, 3]), ALU.mult))
            wait(dve, "u1")
            for y in range(6 * PIECES + 1):
                x, j = y // 6, y % 6
                if y < 6 * PIECES:
                    dve.wait_ge(lin, y + 1)
                    link(dve.scalar_tensor_tensor(u[:, y % 2, :], S[:, 1, piece(x)], u1[:, j, 1:2], u[:, y % 2, :], ALU.mult, ALU.add))
                    link(dve.scalar_tensor_tensor(u[:, y % 2, :], S[:, 2, piece(x)], u1[:, j, 2:3], u[:, y % 2, :], ALU.mult, ALU.add))
                    dve.scalar_tensor_tensor(h[:, y % 2, :], u[:, y % 2, :], SLOPE, u[:, y % 2, :], ALU.mult, ALU.max).then_inc(lrelued, 1)
                y -= 1
                x, j = y // 6, y % 6
                if y >= 0:
                    dve.wait_ge(lrelued, y + 1)
                    if y:
                        dve.wait_ge(used_h, y)
                    for o in range(3):
                        dst = S[:, o, piece(x)] if j == 5 else p2[:, o, :]
                        if j == 0:
                            last = dve.tensor_scalar(dst, h[:, y % 2, :], w2[:, o, j:j + 1], None, ALU.mult)
                        else:
                            last = dve.scalar_tensor_tensor(dst, h[:, y % 2, :], w2[:, o, j:j + 1], p2[:, o, :], ALU.mult, ALU.add)
                    last.then_inc(used_h, 1)
            dve.wait_ge(used_h, 6 * PIECES)

            def norm(name, width):
                mark(dve.tensor_reduce(partial[:, 0:width], S[:, 0:width, :], AX.X, ALU.add))
                wait(dve, "all" + name)
                mark(dve.tensor_scalar(neg_mean[:, 0:width], SUM[:, 0:width], -1.0 / M_ALL, None, ALU.mult))
                wait(dve, "squares" + name)
                mark(dve.tensor_reduce(partial[:, 0:width], part[:, 0:width, :], AX.X, ALU.add))
                wait(dve, "all_sq" + name)
                mark(dve.tensor_scalar(var[:, 0:width], SUM[:, 0:width], 1.0 / M_ALL, None, ALU.mult))
                wait(dve, "pow" + name)
                g, b = gains[int(name) - 1], shifts[int(name) - 1]
                link(dve.tensor_tensor(gain[:, 0:width], inv[:, 0:width], g[:, 0:width], ALU.mult))
                link(dve.tensor_tensor(shift[:, 0:width], neg_mean[:, 0:width], gain[:, 0:width], ALU.mult))
                mark(dve.tensor_tensor(shift[:, 0:width], shift[:, 0:width], b[:, 0:width], ALU.add))

            norm("2", 3)
            for y in range(3 * PIECES):
                x, o = y // 3, y % 3
                dve.wait_ge(act_g, y + 1)
                dve.scalar_tensor_tensor(h[:, y % 2, :], u[:, y % 2, :], SLOPE, u[:, y % 2, :], ALU.mult, ALU.max).then_inc(lrelued, 1)
                dve.wait_ge(lrelued, 6 * PIECES + y + 1)
                if y:
                    dve.wait_ge(used_g, y)
                if o == 0:
                    last = dve.tensor_scalar(S[:, 0, piece(x)], h[:, y % 2, :], w3[:, o:o + 1], None, ALU.mult)
                else:
                    last = dve.scalar_tensor_tensor(S[:, 0, piece(x)], h[:, y % 2, :], w3[:, o:o + 1], S[:, 0, piece(x)], ALU.mult, ALU.add)
                last.then_inc(used_g, 1)
            dve.wait_ge(used_g, 3 * PIECES)
            norm("3", 1)
            dve.memset(att[:, :, K:KP], 0.0)
            wait(dve, "logit")
            link(dve.scalar_tensor_tensor(S[:, 0, :], S[:, 0, :], SLOPE, S[:, 0, :], ALU.mult, ALU.max))
            logit = S[:, 0, :].rearrange("p (m k) -> p m k", k=K)
            wide = [128, N * NT, K]
            link(dve.tensor_reduce(top[:, :], logit, AX.X, ALU.max))
            mark(dve.tensor_tensor(logit, logit, top[:, :].unsqueeze(2).to_broadcast(wide), ALU.subtract))
            wait(dve, "exp")
            link(dve.tensor_reduce(total[:, :], logit, AX.X, ALU.add))
            link(dve.reciprocal(total[:, :], total[:, :]))
            link(dve.tensor_tensor(att[:, :, 0:K], logit, total[:, :].unsqueeze(2).to_broadcast(wide), ALU.mult))
    keep["att"] = att


GROUPS = 32
LAG_E = 1


def neighbour_sum(nc, dram, keep):
    with ExitStack() as es:
        def sb(name, shape, dt=F32):
            return es.enter_context(nc.sbuf_tensor(name, shape, dt))

        def ps(name, shape, dt=F32):
            return es.enter_context(nc.psum_tensor(name, shape, dt))

        counts = []

        def sem(name):
            counts.append(es.enter_context(nc.semaphore(name)))
            return counts[-1]

        ident = sb("d_ident", [128, 128])
        iota_a = sb("iota_a", [128, 128, GROUPS], BF16)
        iota_j = sb("iota_j", [128, 32, GROUPS], BF16)
        eight_q = sb("eight_q", [128, 1])
        minus_half = sb("d_minus_half", [128, 1])
        nb = sb("nb", [128, NT * KP], U16)
        nb_t = sb("nb_t", [128, NT * KP], U16)
        lo_u = sb("lo_u", [128, NT * KP], U16)
        hi_u = sb("hi_u", [128, NT * KP], U16)
        lo = sb("lo", [128, NT, GROUPS], BF16)
        hj = sb("hj", [128, NT, GROUPS], BF16)
        at_n = sb("at_n", [128, NT * KP])
        at_t = sb("at_t", [128, NT * KP])
        rest = sb("d_rest", [128, 2, NT * KP])
        at3 = sb("at3", [128, 3, NT, GROUPS], BF16)
        oh_a = sb("d_oh_a", [128, 2, 128, GROUPS], BF16)
        oh_j = sb("oh_j", [128, 2, 32, GROUPS], BF16)
        placed = sb("placed", [128, 2, 3, 32, GROUPS], BF16)
        x2 = sb("d_x2", [128, BPB, T])
        y3 = sb("d_y3", [128, BPB, T])
        x2_t = sb("x2_t", [128, NT, 128])
        dense = sb("dense", [128, 8, HALF])
        y = sb("d_y", [128, BPB, T])
        stats = sb("d_stats", [128, 2, 6])
        moments = sb("d_moments", [128, 2])
        rstd = sb("d_rstd", [128, 3])

        DM = ps("DM", [128, 2, 512])
        XT = ps("XT", [128, 2, 512])
        AG = ps("AG", [128, 2, 512])

        consts_in = sem("d_consts_in")
        x2_in = [sem(f"x2_in{u}") for u in range(BPB)]
        y3_in = [sem(f"y3_in{u}") for u in range(BPB)]
        copied_in = sem("copied_in")
        split = sem("d_split")
        at_ready = sem("d_at_ready")
        at3_ready = sem("at3_ready")
        oh_ready = sem("d_oh_ready")
        placed_ready = sem("placed_ready")
        dense_ready = sem("dense_ready")
        dense_copied = sem("dense_copied")
        xt_ready = sem("xt_ready")
        xt_copied = sem("xt_copied")
        summed = sem("summed")
        read_out = sem("read_out")
        y3_added = sem("y3_added")
        moments_ready = sem("d_moments_ready")
        pool_ln = sem("d_pool_ln")
        rstd_ready = sem("d_rstd_ready")
        normed = sem("d_normed")
        out_done = [sem(f"out_done{u}") for u in range(BPB)]
        dstep = sem("d_dstep")
        passed = sem("d_passed")
        CONSTS = [(ident[:, :], "ident"), (iota_a[:, :, :], "iota_a"), (iota_j[:, :, :], "iota_j"), (eight_q[:, :], "eight_q"),
                  (minus_half[:, :], "pow_half")]
        block = es.enter_context(nc.Block())

        @block.sync
        def _(sp):
            for dst, name in CONSTS:
                sp.dma_start(dst, dram[name]).then_inc(consts_in, 16)
            with sp.Fori(0, BODY) as i:
                for u in range(BPB):
                    sp.wait_ge(out_done[u], START + i * 16)
                    sp.dma_start(x2[:, u, :], dram["x2"][i * BPB + u]).then_inc(x2_in[u], 16)
                    sp.dma_start(y3[:, u, :], dram["y3"][i * BPB + u]).then_inc(y3_in[u], 16)

        @block.tensor
        def _(pe):
            pe.wait_ge(consts_in, START + 16 * len(CONSTS))
            with pe.Fori(0, BODY) as i:
                for u in range(BPB):
                    def b(n, k=0):
                        return (i * BPB + u) * n + k

                    pe.wait_ge(x2_in[u], START + (i + 1) * 16)
                    pe.wait_ge(xt_copied, START + b(1))
                    for t in range(NT):
                        last = pe.transpose(XT[:, t // 4, (t % 4) * 128:(t % 4 + 1) * 128], x2[:, u, t * 128:(t + 1) * 128], ident[:, :])
                    last.then_inc(xt_ready, 1)
                    for hh in range(2):
                        for t in range(4 * hh, 4 * hh + 4):
                            pe.wait_ge(oh_ready, START + b(NT, t + 1))
                            pe.wait_ge(placed_ready, START + b(NT, t + 1))
                            for e in range(2):
                                pe.wait_ge(dense_copied, START + (b(2 * NT, 2 * t + e - 1) if (t or e or u) else i * BPB * 2 * NT))
                                for g in range(16 * e, 16 * e + 16):
                                    for part in range(3):
                                        last = pe.matmul(DM[:, e, (g % 16) * 32:(g % 16 + 1) * 32], oh_a[:, t % 2, :, g],
                                                         placed[:, t % 2, part, :, g], start=(part == 0), stop=(part == 2))
                                last.then_inc(dense_ready, 1)
                        if hh == 0:
                            pe.wait_ge(xt_copied, START + b(1, 1))
                        pe.wait_ge(dense_copied, START + b(2 * NT, 8 * hh + 8))
                        pe.wait_ge(read_out, START + (b(2, hh - 1) if (hh or u) else i * BPB * 2))
                        for m in range(8):
                            last = pe.matmul(AG[:, hh, :], x2_t[:, m, :], dense[:, m, :], start=(m == 0), stop=(m == 7))
                        last.then_inc(summed, 1)

        @block.scalar
        def _(act):
            with act.Fori(0, BODY) as i:
                for u in range(BPB):
                    def b(n, k=0):
                        return (i * BPB + u) * n + k

                    act.wait_ge(at_ready, START + b(1))
                    act.activation(at_n[:, :].rearrange("p (n k) -> p n k", k=KP), keep["att"][:, bass.ds((i * BPB + u) * NT, NT), :],
                                   ACT.Identity).then_inc(copied_in, 1)
                    act.wait_ge(xt_ready, START + b(1, 1))
                    act.wait_ge(summed, START + b(2))
                    act.activation(x2_t[:, :, :].rearrange("p t c -> p (t c)"), flat(XT[:, :, :]), ACT.Identity).then_inc(xt_copied, 1)
                    for x in range(2 * NT):
                        t, e = x // 2, x % 2
                        act.wait_ge(dense_ready, START + b(2 * NT, x + 1))
                        if x in (0, NT):
                            act.wait_ge(summed, START + b(2, x // NT))
                        src = DM[:, e, :].rearrange("p (g q m) -> p g q m", q=4, m=8)
                        at0 = (t % 4) * 128 + e * 64
                        dst = dense[:, :, at0:at0 + 64].rearrange("p m (g q) -> p g q m", q=4)
                        act.activation(dst, src, ACT.Identity).then_inc(dense_copied, 1)
                    act.wait_ge(rstd_ready, START + b(1, 1))
                    act.activation(y[:, u, :], y[:, u, :], ACT.Identity, scale=rstd[:, 1:2], bias=rstd[:, 2:3]).then_inc(normed, 1)
                    act.wait_ge(normed, START + b(1, 1))
                    act.dma_start(dram["out"][i * BPB + u], y[:, u, :]).then_inc(out_done[u], 16)
            for u in range(BPB):
                act.wait_ge(out_done[u], START + BODY * 16)

        @block.gpsimd
        def _(pool):
            start_counts(pool, counts)
            with pool.Fori(0, BODY) as i:
                n = 0

                def then(ins, plain=True):
                    nonlocal n
                    n += 1
                    ins.then_inc(split, 1)
                    pool.wait_ge(split, START + i * 6 * BPB + n)
                    pool.sem_inc(passed, 1)

                for u in range(BPB):
                    def b(n, k=0):
                        return (i * BPB + u) * n + k

                    flat3 = at3[:, :, :, :].rearrange("p s t g -> p s (t g)")
                    pool.wait_ge(at_ready, START + b(1, 1))
                    pool.wait_ge(placed_ready, START + b(NT))
                    pool.sem_inc(passed, 1)
                    then(pool.tensor_copy(flat3[:, 0, :], at_t[:, :]))
                    then(pool.tensor_tensor(rest[:, 0, :], at_t[:, :], flat3[:, 0, :], ALU.subtract))
                    then(pool.tensor_copy(flat3[:, 1, :], rest[:, 0, :]))
                    then(pool.tensor_tensor(rest[:, 1, :], rest[:, 0, :], flat3[:, 1, :], ALU.subtract))
                    pool.tensor_copy(flat3[:, 2, :], rest[:, 1, :]).then_inc(at3_ready, 1)
                    pool.wait_ge(y3_in[u], START + (i + 1) * 16)
                    for hh in range(2):
                        pool.wait_ge(read_out, START + b(2, hh + 1))
                        half = slice(hh * HALF, (hh + 1) * HALF)
                        pool.tensor_tensor(y[:, u, half], y[:, u, half], y3[:, u, half], ALU.add).then_inc(y3_added, 1)
                    pool.wait_ge(moments_ready, START + b(1, 1))
                    pool.wait_ge(normed, START + b(1))
                    pool.sem_inc(passed, 1)
                    then(pool.tensor_scalar(rstd[:, 0:1], moments[:, 1:2], 1.0, EPS, ALU.mult, ALU.add))
                    then(pool.tensor_tensor(rstd[:, 1:2], rstd[:, 0:1], minus_half[:, :], ALU.pow))
                    pool.tensor_scalar(rstd[:, 2:3], moments[:, 0:1], rstd[:, 1:2], -1.0, ALU.mult, ALU.mult).then_inc(rstd_ready, 1)

        @block.vector
        def _(dve):
            dve.wait_ge(consts_in, START + 16 * len(CONSTS))
            with dve.Fori(0, BODY) as i:
                n = 0

                def link(ins, plain=False):
                    nonlocal n
                    n += 1
                    ins.then_inc(dstep, 1)
                    dve.wait_ge(dstep, START + i * D_STEPS + n)
                    if plain:
                        dve.sem_inc(passed, 1)

                for u in range(BPB):
                    def b(n, k=0):
                        return (i * BPB + u) * n + k

                    link(dve.tensor_copy(nb[:, :], keep["nbr"][:, bass.ds(i * BPB + u, 1), :].rearrange("p u k -> p (u k)")))
                    link(dve.transpose(nb_t[:, :], nb[:, :]))
                    link(dve.tensor_scalar(lo_u[:, :], nb_t[:, :], 127, None, ALU.bitwise_and))
                    link(dve.tensor_scalar(hi_u[:, :], nb_t[:, :], 7, None, ALU.logical_shift_right))
                    dve.tensor_copy(lo[:, :, :].rearrange("p t g -> p (t g)"), lo_u[:, :])
                    link(dve.tensor_scalar(hj[:, :, :].rearrange("p t g -> p (t g)"), hi_u[:, :], eight_q[:, 0:1], None, ALU.add))
                    dve.wait_ge(copied_in, START + b(1, 1))
                    dve.wait_ge(at3_ready, START + b(1))
                    dve.transpose(at_t[:, :], at_n[:, :]).then_inc(at_ready, 1)
                    for t in range(NT + 1):
                        if t < NT:
                            dve.wait_ge(dense_ready, START + (b(2 * NT, 2 * (t - 1)) if (t or u) else i * BPB * 2 * NT))
                            wide = [128, 128, GROUPS]
                            dve.tensor_tensor(oh_a[:, t % 2, :, :], lo[:, t:t + 1, :].to_broadcast(wide), iota_a[:, :, :], ALU.is_equal).then_inc(oh_ready, 1)
                            wide = [128, 32, GROUPS]
                            link(dve.tensor_tensor(oh_j[:, t % 2, :, :], hj[:, t:t + 1, :].to_broadcast(wide), iota_j[:, :, :], ALU.is_equal))
                            if t == 0:
                                dve.wait_ge(at3_ready, START + b(1, 1))
                            for part in range(3):
                                last = dve.tensor_tensor(placed[:, t % 2, part, :, :], oh_j[:, t % 2, :, :],
                                                         at3[:, part, t:t + 1, :].to_broadcast(wide), ALU.mult)
                            last.then_inc(placed_ready, 1)
                        if t in (4 + LAG_E, NT):
                            hh = 0 if t < NT else 1
                            dve.wait_ge(summed, START + b(2, hh + 1))
                            if hh == 0:
                                dve.wait_ge(out_done[u], START + i * 16)
                            half = slice(hh * HALF, (hh + 1) * HALF)
                            view = "p (t q g) -> p t g q"
                            dve.tensor_tensor(y[:, u, half].rearrange(view, q=4, g=GROUPS), AG[:, hh, :].rearrange("p (t g q) -> p t g q", q=4, g=GROUPS),
                                              x2[:, u, half].rearrange(view, q=4, g=GROUPS), ALU.add).then_inc(read_out, 1)
                    dve.wait_ge(y3_added, START + b(2, 2))
                    dve.bn_stats(stats[:, 0, :], y[:, u, 0:HALF])
                    link(dve.bn_stats(stats[:, 1, :], y[:, u, HALF:T]))
                    dve.wait_ge(rstd_ready, START + b(1))
                    dve.sem_inc(passed, 1)
                    dve.bn_aggr(moments[:, :], stats[:, :, :]).then_inc(moments_ready, 1)
                assert n == D_STEPS, n


D_STEPS = BPB * (5 + NT + 1)


def build(nc, dram):
    with ExitStack() as es:
        keep = {"nbr": es.enter_context(nc.sbuf_tensor("nbr_all", [128, N, NT * KP], U16)),
                "pts": es.enter_context(nc.sbuf_tensor("pts_all", [128, N, 3 * NT], F32))}
        attention_and_neighbours(nc, dram, keep)
        keep["sph"] = es.enter_context(nc.sbuf_tensor("sph_all", [128, 3, N, NF], F32))
        spherical_features(nc, dram, keep)
        batch_norms(nc, dram, keep)
        neighbour_sum(nc, dram, keep)


def high_bits(a):
    return (np.asarray(a, np.float32).view(np.uint32) >> 16).astype(np.uint16)


def widened(bits):
    return (np.asarray(bits).astype(np.uint32) << 16).view(np.float32)


def constants():
    out = {"ident": np.eye(128, dtype=np.float32)}
    hm = np.zeros((C, 4, 2), np.float32)
    for c in range(C):
        h = c // DH
        hm[c, 2 * (h // 4) + h % 2, (h // 2) % 2] = DH ** -0.5
    out["head_mask"] = hm.reshape(C, 8)
    pick = np.zeros((96, 128), np.float32)
    pick[[0, 32, 64]] = 1.0
    out["pick3"] = high_bits(pick)
    out["ones3"] = high_bits(np.ones((3, 128)))
    left, parts = np.float32(-1e9), []
    for _ in range(3):
        parts.append(widened(high_bits(left)))
        left = left - parts[-1]
    assert left == 0
    out["neg3"] = np.array(parts, np.float32).reshape(3, 1)
    out["half_neg"] = np.full((128, 128), -0.5, np.float32)
    out["pow_half"] = np.full((128, 1), -0.5, np.float32)
    out["perm3"] = np.eye(128, dtype=np.float32)[:, [0, 2, 1]]
    out["ident_b"] = high_bits(np.eye(128))
    a = np.arange(128)
    pk = np.zeros((98, K, 128), np.float32)
    high_sq = widened(high_bits(a * a))
    for k in range(K):
        pk[k, k] = -2.0 * a
        pk[32 + k, k] = 1.0
        pk[64 + k, k] = 1.0
        pk[96, k] = high_sq
        pk[97, k] = a * a - high_sq
    out["pick_k"] = high_bits(pk)
    out["iota8"] = np.tile(np.arange(8, dtype=np.float32), (128, 1))
    out["iota_a"] = high_bits(np.tile(np.arange(128, dtype=np.float32)[None, :, None], (128, 1, 32)))
    out["iota_j"] = high_bits(np.tile(np.arange(32, dtype=np.float32)[None, :, None], (128, 1, 32)))
    out["eight_q"] = (8 * (np.arange(128, dtype=np.float32) // 32)).reshape(128, 1)
    return out


_LAYER_NAMES = ["L0_xattn", "L1_xattn", "L3_xattn"]


def kernel(**inputs):
    import concourse.bacc as _bacc
    from concourse.bass_utils import run_bass_kernel_spmd as _run

    nc = _bacc.Bacc("TRN2", target_bir_lowering=False, num_devices=1)
    arrays, dram = {}, {}

    def given(name, a):
        a = np.ascontiguousarray(a)
        arrays[f"in_{name}"] = a
        return nc.dram_tensor(f"in_{name}", a.shape, mybir.dt.from_np(a.dtype), kind="ExternalInput").ap()

    dram["x"] = given("x", inputs["x"])
    dram["ctx"] = given("ctx", inputs["ctx_4096"])
    dram["mask"] = given("mask", inputs["mask_Bx1x4096_ff1"])
    dram["w_in"] = [given(f"{l}_w_in", np.asarray(inputs[f"{l}_W_in"]).T) for l in _LAYER_NAMES]
    dram["w_out"] = [given(f"{l}_w_out", np.asarray(inputs[f"{l}_W_out"]).T) for l in _LAYER_NAMES]
    dram["b_in"] = [given(f"{l}_b_in", np.asarray(inputs[f"{l}_b_in"]).reshape(3, C).T) for l in _LAYER_NAMES]
    dram["b_out"] = [given(f"{l}_b_out", np.asarray(inputs[f"{l}_b_out"]).reshape(C, 1)) for l in _LAYER_NAMES]
    for name in ("W1", "W2", "W3", "g1", "g2", "g3", "b1", "b2", "b3"):
        dram[name] = given(name, np.asarray(inputs[f"L2_xattn_{name}"]).reshape(1, -1))
    for name, a in constants().items():
        dram[name] = given(name, a)
        if a.dtype == np.uint16:
            dram[name] = dram[name].bitcast(BF16)
    dram["x2"] = nc.dram_tensor("x2_scratch", (N, C, T), F32, kind="Internal").ap()
    dram["y3"] = nc.dram_tensor("y3_scratch", (N, C, T), F32, kind="Internal").ap()
    dram["out"] = nc.dram_tensor("out", (N, C, T), F32, kind="ExternalOutput").ap()
    build(nc, dram)
    r = _run(nc, [arrays], core_ids=[0])
    return r.results[0]["out"]
```

```python
from contextlib import ExitStack

import numpy as np
import concourse.bass as bass
from concourse import mybir

F32 = mybir.dt.float32
BF16 = mybir.dt.bfloat16
U16 = mybir.dt.uint16
ALU = mybir.AluOpType
ACT = mybir.ActivationFunctionType
AX = mybir.AxisListType

N, C, T = 32, 128, 1024
H, DH, CHUNK = 8, 16, 64
NT = T // 128
K, KP = 30, 32
ROUNDS = KP // 8
EPS = 1e-5
TINY = 1e-20
NEG_BIG = -3.0e38
LAYERS = 3
BPB = 4
BODY = N // BPB
BPD = 2
BODY_D = N // BPD
PAIRS = T // (2 * CHUNK)
STEPS = BPB * LAYERS * PAIRS
PASSES = BPB * LAYERS
TILES = BPB * NT
SPAN = STEPS // TILES
HALF = T // 2

LAG_SUM, LAG_T, LAG_PV, LAG_O, LAG_Y = 1, 3, 4, 5, 6
LAG_BN, LAG_LN, LAG_ST = 7, 8, 9
TAIL = LAG_ST
ORDER = range(STEPS + TAIL)


PARTS = [("q", 0), ("q", 1), ("k", 0), ("k", 1), ("v", 0), ("v", 1)]


def squares_at(s):
    batch = (s + 1) // (LAYERS * PAIRS)
    starts = s == 0 or ((s + 1) % (LAYERS * PAIRS) == 0 and batch < BPB)
    return [0 if s == 0 else batch] if starts else []


def projections_at(s):
    if s == 0:
        return [(what, 0, h) for what, h in PARTS]
    w, part = (s + len(PARTS)) // PAIRS, (s + len(PARTS)) % PAIRS
    return [(PARTS[part][0], w, PARTS[part][1])] if 1 <= w < PASSES and part < len(PARTS) else []


def psum_uses():
    uses = []
    for s in ORDER:
        uses += [("xx", u, h) for u in squares_at(s) for h in range(3)]
        uses += projections_at(s)
        h = s - LAG_O
        if 0 <= h < STEPS and h % 4 == 3:
            uses.append(("y", h // PAIRS, (h % PAIRS) // 4))
    return uses


USES = psum_uses()
USE = {u: n for n, u in enumerate(USES)}
NUSE = len(USES)
assert NUSE % 2 == 0


def flat(ap):
    return ap.rearrange("p a b -> p (a b)")


START = 1


def start_counts(pool, counts):
    for count in counts:
        pool.sem_inc(count, START)


def attention_and_neighbours(nc, dram, keep):
    per_dv = [0]
    with ExitStack() as es:
        def sb(name, shape, dt=F32):
            return es.enter_context(nc.sbuf_tensor(name, shape, dt))

        def ps(name, shape, dt=F32):
            return es.enter_context(nc.psum_tensor(name, shape, dt))

        counts = []

        def sem(name):
            counts.append(es.enter_context(nc.semaphore(name)))
            return counts[-1]

        ident = sb("ident", [128, 128])
        head_mask = sb("head_mask", [128, 8])
        pick3 = sb("pick3", [96, 128], BF16)
        ones3 = sb("ones3", [3, 128], BF16)
        neg3 = sb("neg3", [3, 1])
        half_neg = sb("half_neg", [128, 128])
        w_in = sb("w_in", [128, LAYERS, 3 * C])
        w_out = sb("w_out", [128, LAYERS, C])
        b_in = sb("b_in", [128, LAYERS, 3])
        b_out = sb("b_out", [128, LAYERS])
        pow_half = sb("pow_half", [128, 1])
        perm3 = sb("perm3", [128, 3])
        ctx = sb("ctx", [128, BPB, T])
        xb = sb("xb", [128, BPB, T])
        mask = sb("mask", [128, BPB, T])
        sq = sb("sq", [128, T])
        vrow = sb("vrow", [128, T])
        rest = sb("rest", [128, T])
        dist_row = sb("dist_row", [96, T], BF16)
        mask_row = sb("mask_row", [3, T], BF16)
        xcol = sb("xcol", [128, BPB, 32])
        q_t = sb("q_t", [128, 2, T])
        k_t = sb("k_t", [128, 2, T])
        v_b = sb("v_b", [128, 2, 16, 128])
        q_bd = sb("q_bd", [128, 2, 2, 512])
        prob = sb("prob", [128, 4, 512])
        prob_t = sb("prob_t", [128, 2, 512])
        row_max = sb("row_max", [128, 2, 8])
        row_sum = sb("row_sum", [128, 2, 8])
        row_rec = sb("row_rec", [128, 2, 8])
        o_t = sb("o_t", [128, 2, HALF])
        y_b = sb("y_b", [128, LAYERS, T])
        stats = sb("stats", [128, 2, 6])
        moments = sb("moments", [128, 2, 2])
        rstd = sb("rstd", [128, 2, 3])
        dist = sb("dist", [128, 2, T])
        top8 = sb("top8", [128, ROUNDS, 8])
        nbr = sb("nbr", [128, BPB, NT, KP], U16)

        PJ = ps("PJ", [128, 2, 512])
        PD = ps("PD", [128, 2, 512])
        SC = ps("SC", [128, 2, 512])
        PT = ps("PT", [128, 512])
        OP = ps("OP", [128, 2, 128])

        consts_in = sem("consts_in")
        zeroed = sem("zeroed")
        ctx_in = [sem(f"ctx_in{u}") for u in range(BPB)]
        x_in = [sem(f"x_in{u}") for u in range(BPB)]
        mask_in = [sem(f"mask_in{u}") for u in range(BPB)]
        pj_ready = sem("pj_ready")
        pj_free = [sem(f"pj_free{b}") for b in range(2)]
        squared = sem("squared")
        col_ready = sem("col_ready")
        row_ready = sem("row_ready")
        pool_split = sem("pool_split")
        dist_row_ready = sem("dist_row_ready")
        mask_row_ready = sem("mask_row_ready")
        qbd_ready = sem("qbd_ready")
        scored = sem("scored")
        maxed = sem("maxed")
        exped = sem("exped")
        recip_ready = sem("recip_ready")
        normed = sem("normed")
        transposed = sem("transposed")
        pt_ready = sem("pt_ready")
        pv_ready = sem("pv_ready")
        o_ready = sem("o_ready")
        masked = sem("masked")
        added = sem("added")
        moments_ready = sem("moments_ready")
        pool_ln = sem("pool_ln")
        rstd_ready = sem("rstd_ready")
        applied = [sem(f"applied{j}") for j in range(2)]
        x2_out = [sem(f"x2_out{u}") for u in range(BPB)]
        y3_out = sem("y3_out")
        pd_ready = sem("pd_ready")
        pd_copied = sem("pd_copied")
        topped = sem("topped")
        dve_step = sem("dve_step")
        passed = sem("passed")

        CONSTS = [(ident, dram["ident"]), (head_mask, dram["head_mask"]), (pick3, dram["pick3"]), (ones3, dram["ones3"]),
                  (neg3, dram["neg3"]), (half_neg, dram["half_neg"]), (pow_half, dram["pow_half"]), (perm3, dram["perm3"])]
        NCONST = len(CONSTS) + 4 * LAYERS

        def copied(eng, i, use):
            n = USE[use]
            eng.wait_ge(pj_free[n % 2], START + i * (NUSE // 2) + n // 2 + 1)

        def alone(eng):
            eng.sem_inc(passed, 1)

        block = es.enter_context(nc.Block())

        @block.sync
        def _(sp):
            for tile, src in CONSTS:
                sp.dma_start(tile[:, :], src).then_inc(consts_in, 16)
            for j in range(LAYERS):
                sp.dma_start(w_in[:, j, :], dram["w_in"][j]).then_inc(consts_in, 16)
                sp.dma_start(w_out[:, j, :], dram["w_out"][j]).then_inc(consts_in, 16)
                sp.dma_start(b_in[:, j, :], dram["b_in"][j]).then_inc(consts_in, 16)
                sp.dma_start(b_out[:, j:j + 1], dram["b_out"][j]).then_inc(consts_in, 16)
            with sp.Fori(0, BODY) as i:
                for u in range(BPB):
                    sp.wait_ge(pd_ready, START + i * TILES + NT * (u + 1))
                    sp.dma_start(ctx[:, u, :], dram["ctx"][i * BPB + u]).then_inc(ctx_in[u], 16)
                    sp.wait_ge(masked, START + i * BPB + u + 1)
                    sp.dma_start(mask[:, u, :], dram["mask"][i * BPB + u].broadcast_to([128, T])).then_inc(mask_in[u], 16)
                    sp.wait_ge(x2_out[u], START + i * 16)
                    sp.dma_start(xb[:, u, :], dram["x"][i * BPB + u]).then_inc(x_in[u], 16)


        @block.tensor
        def _(pe):
            pe.sem_inc(pd_ready, TILES)
            pe.wait_ge(consts_in, START + 16 * NCONST)
            pe.wait_ge(zeroed, START + 2)
            with pe.Fori(0, BODY) as i:
                def claim(use):
                    n = USE[use]
                    pe.wait_ge(pj_free[n % 2], START + i * (NUSE // 2) + n // 2)
                    return PJ[:, n % 2, :]

                for s in ORDER:
                    u, w, p = s // (LAYERS * PAIRS), s // PAIRS, s % PAIRS
                    c = w % 2
                    for ub in squares_at(s):
                        pe.wait_ge(squared, START + i * BPB + ub + 1)
                        for h in range(2):
                            bank = claim(("xx", ub, h))
                            pe.matmul(bank, half_neg[:, :], sq[:, h * HALF:(h + 1) * HALF], start=True, stop=True).then_inc(pj_ready, 1)
                        bank = claim(("xx", ub, 2))
                        pe.wait_ge(ctx_in[ub], START + (i + 1) * 16)
                        for t in range(NT):
                            pe.matmul(bank[:, 8 + 3 * t:11 + 3 * t], ctx[:, ub, t * 128:(t + 1) * 128], perm3[:, :], start=True, stop=True)
                        for t in range(NT):
                            last = pe.matmul(bank[:, t:t + 1], sq[:, t * 128:(t + 1) * 128], half_neg[:, 0:1], start=True, stop=True)
                        last.then_inc(pj_ready, 1)
                    for name, pw, h in projections_at(s):
                        pu, pj = pw // LAYERS, pw % LAYERS
                        pe.wait_ge(ctx_in[pu], START + (i + 1) * 16)
                        bank = claim((name, pw, h))
                        if name != "v":
                            n = "qk".index(name)
                            pe.matmul(bank, w_in[:, pj, n * C:(n + 1) * C], ctx[:, pu, h * HALF:(h + 1) * HALF],
                                      start=True, stop=True).then_inc(pj_ready, 1)
                        else:
                            w_v = w_in[:, pj, 2 * C:3 * C].rearrange("p (g e d) -> p e g d", g=4, e=2)
                            for m in range(8):
                                t0 = (8 * h + m) * CHUNK
                                for e in range(2):
                                    last = pe.matmul(bank[64 * e:64 * e + 64, m * 64:(m + 1) * 64], ctx[:, pu, t0:t0 + CHUNK],
                                                     w_v[:, e, :, :], start=True, stop=True)
                            last.then_inc(pj_ready, 1)
                    if s < STEPS and s % SPAN == 0:
                        tt = s // SPAN
                        t = tt % NT
                        pe.wait_ge(dist_row_ready, START + i * BPB + u + 1)
                        pe.wait_ge(pd_copied, START + i * TILES + tt)
                        for h in range(2):
                            pe.matmul(PD[:, h, :], pick3[:, :], dist_row[:, h * HALF:(h + 1) * HALF], start=True, stop=False)
                            last = pe.matmul(PD[:, h, :], ctx[:, u, t * 128:(t + 1) * 128], ctx[:, u, h * HALF:(h + 1) * HALF],
                                             start=False, stop=True)
                        last.then_inc(pd_ready, 1)
                    if s < STEPS:
                        bank = SC[:, s % 2, :].rearrange("p (c h k) -> p c h k", c=2, h=4)
                        if p == 0:
                            pe.wait_ge(mask_row_ready, START + i * BPB + u + 1)
                            copied(pe, i, ("v", w, 0))
                            copied(pe, i, ("v", w, 1))
                        pe.wait_ge(exped, START + i * STEPS + max(s - 1, 0))
                        pe.wait_ge(qbd_ready, START + i * STEPS + s + 1)
                        toks = p * 2 * CHUNK
                        rows = mask_row[:, toks:toks + 2 * CHUNK].rearrange("p (c k) -> p c k", c=2).unsqueeze(2).to_broadcast([3, 2, 4, CHUNK])
                        pe.matmul(bank, ones3[:, :], rows, start=True, stop=False, skip_group_check=True)
                        for ch in range(2):
                            for hp in range(4):
                                last = pe.matmul(bank[:, ch, hp, :], q_bd[:, s % 2, ch, hp * 128:(hp + 1) * 128],
                                                 k_t[:, c, toks + ch * CHUNK:toks + (ch + 1) * CHUNK], start=False, stop=True, skip_group_check=True)
                        last.then_inc(scored, 1)
                    r = s - LAG_T
                    if 0 <= r < STEPS:
                        pe.wait_ge(normed, START + i * STEPS + r + 1)
                        pe.wait_ge(pt_ready, START + i * STEPS + r)
                        for m in range(4):
                            last = pe.transpose(PT[:, m * 128:(m + 1) * 128], prob[:, r % 4, m * 128:(m + 1) * 128], ident[:, :])
                        last.then_inc(transposed, 1)
                    r = s - LAG_PV
                    if 0 <= r < STEPS:
                        pe.wait_ge(pt_ready, START + i * STEPS + r + 1)
                        pe.wait_ge(o_ready, START + i * STEPS + r)
                        for ch in range(2):
                            for a in range(2):
                                for b in range(2):
                                    g = 2 * a + b
                                    last = pe.matmul(OP[32 * g:32 * g + 32, r % 2, ch * CHUNK:(ch + 1) * CHUNK],
                                                     v_b[:, (r // PAIRS) % 2, 2 * (r % PAIRS) + ch, 32 * g:32 * g + 32],
                                                     prob_t[:, r % 2, (2 * ch + a) * 128 + b * 64:(2 * ch + a) * 128 + b * 64 + 64],
                                                     start=True, stop=True)
                        last.then_inc(pv_ready, 1)
                    r = s - LAG_O
                    if 0 <= r < STEPS and r % 4 == 3:
                        bank = claim(("y", r // PAIRS, (r % PAIRS) // 4))
                        pe.wait_ge(o_ready, START + i * STEPS + r + 1)
                        pe.matmul(bank, w_out[:, (r // PAIRS) % LAYERS, :], o_t[:, (r // 4) % 2, :], start=True, stop=True).then_inc(pj_ready, 1)

        @block.scalar
        def _(act):
            act.wait_ge(consts_in, START + 16 * NCONST)
            act.wait_ge(zeroed, START + 2)
            with act.Fori(0, BODY) as i:
                def produced(use):
                    n = USE[use]
                    act.wait_ge(pj_ready, START + i * NUSE + n + 1)
                    return PJ[:, n % 2, :], pj_free[n % 2]

                for s in ORDER:
                    u, w, p = s // (LAYERS * PAIRS), s // PAIRS, s % PAIRS
                    c = w % 2
                    for ub in squares_at(s):
                        act.wait_ge(ctx_in[ub], START + (i + 1) * 16)
                        act.wait_ge(pj_ready, START + (i * NUSE + (USE[("xx", ub - 1, 2)] + 1 if ub else 0)))
                        act.activation(sq[:, :], ctx[:, ub, :], ACT.Square).then_inc(squared, 1)
                        act.wait_ge(dist_row_ready, START + i * BPB + ub)
                        for h in range(2):
                            bank, free = produced(("xx", ub, h))
                            act.activation(vrow[:, h * HALF:(h + 1) * HALF], bank, ACT.Identity).then_inc(free, 1)
                        bank, free = produced(("xx", ub, 2))
                        act.activation(xcol[:, ub, :], bank[:, 0:32], ACT.Identity, scale=2.0).then_inc(free, 1)
                        copied(act, i, ("xx", ub, 2))
                        act.activation(keep["pts"][:, bass.ds(i * BPB + ub, 1), :], xcol[:, ub:ub + 1, 8:32], ACT.Identity, scale=0.5).then_inc(col_ready, 1)
                    for name, pw, h in projections_at(s):
                        done = max(PAIRS * (pw - 1), 0)
                        if name != "v":
                            act.wait_ge(scored, START + i * STEPS + done)
                            act.wait_ge(qbd_ready, START + i * STEPS + done)
                            bank, free = produced((name, pw, h))
                            dst, n = (q_t, 0) if name == "q" else (k_t, 1)
                            act.activation(dst[:, pw % 2, h * HALF:(h + 1) * HALF], bank, ACT.Identity, bias=b_in[:, pw % LAYERS, n:n + 1]).then_inc(free, 1)
                        else:
                            act.wait_ge(pv_ready, START + i * STEPS + done)
                            bank, free = produced((name, pw, h))
                            for e in range(2):
                                src = bank[64 * e:64 * e + 64, :].rearrange("p (m d) -> p m d", d=DH)
                                dst = v_b[64 * e:64 * e + 64, pw % 2, 8 * h:8 * h + 8, :].rearrange("p m (g e d) -> p (m g) e d", g=4, e=2)[:, :, e, :]
                                last = act.activation(dst, src, ACT.Identity)
                            last.then_inc(free, 1)
                    if s < STEPS and s % SPAN == 0:
                        tt = s // SPAN
                        act.wait_ge(pd_ready, START + TILES + i * TILES + tt + 1)
                        act.wait_ge(topped, START + i * TILES + max(tt - 1, 0))
                        act.activation(dist[:, tt % 2, :], flat(PD[:, :, :]), ACT.Identity, scale=2.0,
                                       bias=xcol[:, u, tt % NT:tt % NT + 1]).then_inc(pd_copied, 1)
                    if s < STEPS:
                        act.wait_ge(maxed, START + i * STEPS + s + 1)
                        act.wait_ge(transposed, START + i * STEPS + max(s - 3, 0))
                        act.wait_ge(recip_ready, START + i * STEPS + max(s - 1, 0))
                        for g in range(8):
                            last = act.activation(prob[:, s % 4, g * CHUNK:(g + 1) * CHUNK], SC[:, s % 2, g * CHUNK:(g + 1) * CHUNK], ACT.Exp,
                                                  bias=row_max[:, s % 2, g:g + 1], accum_out=row_sum[:, s % 2, g:g + 1])
                        last.then_inc(exped, 1)
                    r = s - LAG_T
                    if 0 <= r < STEPS:
                        act.wait_ge(transposed, START + i * STEPS + r + 1)
                        act.wait_ge(pv_ready, START + i * STEPS + max(r - 1, 0))
                        act.activation(prob_t[:, r % 2, :], PT[:, :], ACT.Identity).then_inc(pt_ready, 1)
                    r = s - LAG_PV
                    if 0 <= r < STEPS:
                        act.wait_ge(pv_ready, START + i * STEPS + r + 1)
                        if r % 4 == 0:
                            before = USE[("y", (r // 4 - 2) // 2, r // 4 % 2)] + 1 if r // 4 >= 2 else 0
                            act.wait_ge(pj_ready, START + i * NUSE + before)
                        act.activation(o_t[:, (r // 4) % 2, (r % 4) * 128:(r % 4 + 1) * 128], OP[:, r % 2, :], ACT.Identity,
                                       bias=b_in[:, (r // PAIRS) % LAYERS, 2:3]).then_inc(o_ready, 1)
                    r = s - LAG_LN
                    if 0 <= r < STEPS and r % PAIRS == PAIRS - 1 and (r // PAIRS) % LAYERS < 2:
                        jj, uu = (r // PAIRS) % LAYERS, r // (LAYERS * PAIRS)
                        act.wait_ge(rstd_ready, START + i * 2 * BPB + 2 * uu + jj + 1)
                        act.activation(xb[:, uu, :], y_b[:, jj, :], ACT.Identity, scale=rstd[:, jj, 1:2], bias=rstd[:, jj, 2:3]).then_inc(applied[jj], 1)
                    r = s - LAG_ST
                    if 0 <= r < STEPS and r % PAIRS == PAIRS - 1:
                        jj, uu = (r // PAIRS) % LAYERS, r // (LAYERS * PAIRS)
                        if jj == 1:
                            act.wait_ge(applied[1], START + i * BPB + uu + 1)
                            act.dma_start(dram["x2"][i * BPB + uu], xb[:, uu, :]).then_inc(x2_out[uu], 16)
                        if jj == 2:
                            act.wait_ge(masked, START + BPB + i * BPB + uu + 1)
                            act.dma_start(dram["y3"][i * BPB + uu], y_b[:, 2, :]).then_inc(y3_out, 16)
            for u in range(BPB):
                act.wait_ge(x2_out[u], START + BODY * 16)
            act.wait_ge(y3_out, START + N * 16)

        @block.gpsimd
        def _(pool):
            start_counts(pool, counts)
            pool.memset(v_b[:, 0, :, :], 0.0).then_inc(zeroed, 1)
            pool.memset(v_b[:, 1, :, :], 0.0).then_inc(zeroed, 1)
            pool.wait_ge(consts_in, START + 16 * NCONST)
            with pool.Fori(0, BODY) as i:
                split = 0
                lnstep = 0
                for s in ORDER:
                    for ub in squares_at(s):
                        pool.wait_ge(col_ready, START + i * BPB + ub + 1)
                        pool.wait_ge(pd_ready, START + TILES + i * TILES + NT * ub)
                        pool.wait_ge(normed, START + i * STEPS + max(s - LAG_SUM, 0))
                        pool.wait_ge(qbd_ready, START + i * STEPS + (s + 1 if s else 0))
                        pool.wait_ge(rstd_ready, START + i * 2 * BPB + 2 * ub)
                        pool.wait_ge(added, START + i * 4 * BPB + 4 * ub)
                        alone(pool)

                        def then(ins):
                            nonlocal split
                            split += 1
                            ins.then_inc(pool_split, 1)
                            pool.wait_ge(pool_split, START + i * SPLITS + split)
                            alone(pool)

                        then(pool.tensor_copy(dist_row[0:96, :], vrow[0:96, :]))
                        then(pool.tensor_tensor(rest[0:96, :], vrow[0:96, :], dist_row[0:96, :], ALU.subtract))
                        then(pool.tensor_copy(dist_row[32:64, :], rest[32:64, :]))
                        then(pool.tensor_copy(dist_row[64:96, :], rest[64:96, :]))
                        then(pool.tensor_tensor(rest[64:96, :], rest[64:96, :], dist_row[64:96, :], ALU.subtract))
                        pool.tensor_copy(dist_row[64:96, :], rest[64:96, :]).then_inc(dist_row_ready, 1)
                        pool.wait_ge(dist_row_ready, START + i * BPB + ub + 1)
                    for q in ([0] if s == 0 else []) + ([s + 1] if s + 1 < STEPS else []):
                        qw, qp = q // PAIRS, q % PAIRS
                        if qp == 0:
                            copied(pool, i, ("q", qw, 0))
                            copied(pool, i, ("q", qw, 1))
                        pool.wait_ge(scored, START + i * STEPS + max(q - 1, 0))
                        for ch in range(2):
                            t0 = (2 * qp + ch) * CHUNK
                            qq = q_t[:, qw % 2, t0:t0 + CHUNK].unsqueeze(1).to_broadcast([128, 8, CHUNK])
                            hm = head_mask[:, :].unsqueeze(2).to_broadcast([128, 8, CHUNK])
                            last = pool.tensor_tensor(q_bd[:, q % 2, ch, :].rearrange("p (h k) -> p h k", h=8), qq, hm, ALU.mult)
                        last.then_inc(qbd_ready, 1)
                    r = s - LAG_SUM
                    if 0 <= r < STEPS:
                        pool.wait_ge(recip_ready, START + i * STEPS + r + 1)
                        pr = prob[:, r % 4, :].rearrange("p (h k) -> p h k", h=8)
                        pool.tensor_tensor(pr, pr, row_rec[:, r % 2, :].unsqueeze(2).to_broadcast([128, 8, CHUNK]), ALU.mult).then_inc(normed, 1)
                    r = s - LAG_Y
                    if 0 <= r < STEPS and r % 4 == 3 and (r // PAIRS) % LAYERS < 2:
                        jj, uu, h = (r // PAIRS) % LAYERS, r // (LAYERS * PAIRS), (r % PAIRS) // 4
                        copied(pool, i, ("y", r // PAIRS, h))
                        if jj == 0:
                            pool.wait_ge(x_in[uu], START + (i + 1) * 16)
                        else:
                            pool.wait_ge(applied[0], START + i * BPB + uu + 1)
                        half = slice(h * HALF, (h + 1) * HALF)
                        pool.tensor_tensor(y_b[:, jj, half], y_b[:, jj, half], xb[:, uu, half], ALU.add).then_inc(added, 1)
                    r = s - LAG_BN
                    if 0 <= r < STEPS and r % PAIRS == PAIRS - 1 and (r // PAIRS) % LAYERS < 2:
                        jj, uu = (r // PAIRS) % LAYERS, r // (LAYERS * PAIRS)
                        pool.wait_ge(moments_ready, START + i * 2 * BPB + 2 * uu + jj + 1)
                        pool.wait_ge(applied[jj], START + i * BPB + uu)
                        alone(pool)
                        pool.tensor_scalar(rstd[:, jj, 0:1], moments[:, jj, 1:2], 1.0, EPS, ALU.mult, ALU.add).then_inc(pool_ln, 1)
                        pool.wait_ge(pool_ln, START + i * 4 * BPB + lnstep + 1)
                        pool.tensor_tensor(rstd[:, jj, 1:2], rstd[:, jj, 0:1], pow_half[:, :], ALU.pow).then_inc(pool_ln, 1)
                        pool.wait_ge(pool_ln, START + i * 4 * BPB + lnstep + 2)
                        alone(pool)
                        pool.tensor_scalar(rstd[:, jj, 2:3], moments[:, jj, 0:1], rstd[:, jj, 1:2], -1.0, ALU.mult, ALU.mult).then_inc(rstd_ready, 1)
                        lnstep += 2
                assert split == SPLITS and lnstep == 4 * BPB

        @block.vector
        def _(dve):
            dve.sem_inc(masked, BPB)
            dve.wait_ge(consts_in, START + 16 * NCONST)
            with dve.Fori(0, BODY) as i:
                def link(ins, plain=False):
                    per_dv[0] += 1
                    ins.then_inc(dve_step, 1)
                    dve.wait_ge(dve_step, START + i * DVE_STEPS + per_dv[0])
                    if plain:
                        alone(dve)

                for s in ORDER:
                    u, w, p = s // (LAYERS * PAIRS), s // PAIRS, s % PAIRS
                    if s < STEPS and s % (LAYERS * PAIRS) == 0:
                        dve.wait_ge(mask_in[u], START + (i + 1) * 16)
                        dve.wait_ge(scored, START + i * STEPS + s)
                        dve.tensor_scalar(mask_row[:, :], mask[0:3, u, :], 0.0, neg3[:, 0:1], ALU.is_le, ALU.mult).then_inc(mask_row_ready, 1)
                    r = s - LAG_SUM
                    if 0 <= r < STEPS:
                        dve.wait_ge(exped, START + i * STEPS + r + 1)
                        dve.wait_ge(normed, START + i * STEPS + max(r - 1, 0))
                        dve.reciprocal(row_rec[:, r % 2, :], row_sum[:, r % 2, :]).then_inc(recip_ready, 1)
                    r = s - LAG_Y
                    if 0 <= r < STEPS and r % 4 == 3:
                        ww, jj, uu, h = r // PAIRS, (r // PAIRS) % LAYERS, r // (LAYERS * PAIRS), (r % PAIRS) // 4
                        n = USE[("y", ww, h)]
                        dve.wait_ge(pj_ready, START + i * NUSE + n + 1)
                        if h == 0:
                            if jj < 2:
                                dve.wait_ge(applied[jj], START + i * BPB + uu)
                            else:
                                dve.wait_ge(y3_out, START + (i * BPB + uu) * 16)
                        half = slice(h * HALF, (h + 1) * HALF)
                        dve.scalar_tensor_tensor(y_b[:, jj, half], PJ[:, n % 2, :], b_out[:, jj:jj + 1], mask[:, uu, half],
                                                 ALU.add, ALU.mult).then_inc(pj_free[n % 2], 1)
                        if jj == LAYERS - 1 and h == 1:
                            copied(dve, i, ("y", ww, 0))
                            copied(dve, i, ("y", ww, 1))
                            dve.sem_inc(masked, 1)
                    if s < STEPS:
                        dve.wait_ge(scored, START + i * STEPS + s + 1)
                        dve.tensor_reduce(row_max[:, s % 2, :], SC[:, s % 2, :].rearrange("p (h k) -> p h k", h=8), AX.X, ALU.max,
                                          negate=True).then_inc(maxed, 1)
                    r = s - LAG_BN
                    if 0 <= r < STEPS and r % PAIRS == PAIRS - 1 and (r // PAIRS) % LAYERS < 2:
                        jj, uu = (r // PAIRS) % LAYERS, r // (LAYERS * PAIRS)
                        dve.wait_ge(added, START + i * 4 * BPB + 4 * uu + 2 * jj + 2)
                        dve.bn_stats(stats[:, 0, :], y_b[:, jj, 0:HALF])
                        link(dve.bn_stats(stats[:, 1, :], y_b[:, jj, HALF:T]), plain=True)
                        dve.bn_aggr(moments[:, jj, :], stats[:, :, :]).then_inc(moments_ready, 1)
                    if 1 <= s <= STEPS:
                        tt, part = (s - 1) // SPAN, (s - 1) % SPAN
                        uu, t = tt // NT, tt % NT
                        if part == 0:
                            dve.wait_ge(pd_copied, START + i * TILES + tt + 1)
                            alone(dve)
                        for k in ((0, 1), (2,), (3,))[part]:
                            link(dve.max(top8[:, k, :], dist[:, tt % 2, :]), plain=True)
                            if k < ROUNDS - 1:
                                dve.max_index(nbr[:, uu, t, k * 8:(k + 1) * 8], top8[:, k, :], dist[:, tt % 2, :])
                                link(dve.match_replace(dist[:, tt % 2, :], top8[:, k, :], dist[:, tt % 2, :], NEG_BIG), plain=True)
                            else:
                                dve.max_index(nbr[:, uu, t, k * 8:(k + 1) * 8], top8[:, k, :], dist[:, tt % 2, :]).then_inc(topped, 1)
                        if part == SPAN - 1 and t == NT - 1:
                            dve.wait_ge(topped, START + i * TILES + tt + 1)
                            link(dve.tensor_copy(keep["nbr"][:, bass.ds(i * BPB + uu, 1), :],
                                            nbr[:, uu:uu + 1, :, :].rearrange("p u t k -> p u (t k)")))
                assert per_dv[0] == DVE_STEPS, per_dv[0]



SPLITS = 5 * BPB
DVE_STEPS = TILES * (2 * ROUNDS - 1) + BPB + 2 * BPB


KQ = 4
QUADS = -(-K // KQ)
DEEP = 3
SPLIT_K = 21
NF = NT * K


def spherical_features(nc, dram, keep):
    with ExitStack() as es:
        def sb(name, shape, dt=F32):
            return es.enter_context(nc.sbuf_tensor(name, shape, dt))

        def ps(name, shape, dt=F32):
            return es.enter_context(nc.psum_tensor(name, shape, dt))

        counts = []

        def sem(name):
            counts.append(es.enter_context(nc.semaphore(name)))
            return counts[-1]

        ident_b = sb("ident_b", [128, 128], BF16)
        pick_k = sb("pick_k", [98, K, 128], BF16)
        iota8 = sb("iota8", [128, 8])
        low_u = sb("low_u", [128, NT * KP], U16)
        high_u = sb("high_u", [128, NT * KP], U16)
        low = sb("low", [128, NT * KP], BF16)
        high = sb("high", [128, NT * KP])
        oh_b = sb("oh_b", [128, NT * KP, 8])
        rows = sb("rows", [98, T], BF16)
        low2 = sb("low2", [32, T])
        low2_b = sb("low2_b", [32, T], BF16)
        own = sb("own", [128, NT, 3])
        table = sb("table", [128, 3, 24], BF16)
        left = sb("left", [128, 2, 24])
        oh_a = sb("oh_a", [128, DEEP, 512], BF16)
        cand = sb("cand", [128, 2, K * 24])
        rel = sb("rel", [128, 3, NT, K])
        apart = sb("apart", [128, 3, NF])
        sqr = sb("sqr", [128, 3, NF])
        r2 = sb("r2", [128, 2, NF])
        r2m = sb("r2m", [128, 2, NF])
        root = sb("root", [128, 2, NF])
        good = sb("good", [128, 2, NF])
        degen = sb("degen", [128, 2, NF])
        yy = sb("yy", [128, 2, NF])
        xx = sb("xx", [128, 2, NF])
        ay = sb("ay", [128, 2, NF])
        ax = sb("ax", [128, 2, NF])
        big = sb("big", [128, 2, NF])
        ratio = sb("ratio", [128, 2, NF])
        at = sb("at", [128, 2, NF])
        flag = sb("flag", [128, 2, NF])
        turn = sb("turn", [128, 2, NF])

        BC = ps("BC", [128, DEEP, 512])
        LT = ps("LT", [32, T], BF16)
        G = ps("G", [128, 2, 2, 512])

        consts_in = sem("b_consts_in")
        low_ready = sem("low_ready")
        lt_ready = sem("lt_ready")
        lt_copied = sem("lt_copied")
        rows_ready = sem("rows_ready")
        own_ready = sem("own_ready")
        table_step = sem("table_step")
        table_ready = sem("table_ready")
        bc_ready = sem("bc_ready")
        oh_ready = sem("oh_ready")
        fetched = sem("fetched")
        g_free = sem("g_free")
        r2_ready = sem("r2_ready")
        root_ready = sem("root_ready")
        yx_ready = sem("yx_ready")
        abs_ready = sem("abs_ready")
        ratio_ready = sem("ratio_ready")
        at_ready = sem("at_ready")
        dstep = sem("b_dstep")
        passed = sem("b_passed")
        NCONST = 3

        block = es.enter_context(nc.Block())

        @block.sync
        def _(sp):
            sp.dma_start(ident_b[:, :], dram["ident_b"]).then_inc(consts_in, 16)
            sp.dma_start(pick_k[:, :, :], dram["pick_k"]).then_inc(consts_in, 16)
            sp.dma_start(iota8[:, :], dram["iota8"]).then_inc(consts_in, 16)
            sp.wait_ge(consts_in, START + 16 * NCONST)

        @block.gpsimd
        def _(pool):
            start_counts(pool, counts)
            with pool.Fori(0, N) as i:
                n = 0

                def then(ins):
                    nonlocal n
                    n += 1
                    ins.then_inc(table_step, 1)
                    pool.wait_ge(table_step, START + i * 4 + n)
                    pool.sem_inc(passed, 1)

                pool.wait_ge(own_ready, START + i + 1)
                pool.wait_ge(fetched, START + i * NT * QUADS)
                pool.sem_inc(passed, 1)
                src = own[:, :, :].rearrange("p t c -> p (t c)")
                then(pool.tensor_copy(table[:, 0, :], src))
                then(pool.tensor_tensor(left[:, 0, :], src, table[:, 0, :], ALU.subtract))
                then(pool.tensor_copy(table[:, 1, :], left[:, 0, :]))
                then(pool.tensor_tensor(left[:, 1, :], left[:, 0, :], table[:, 1, :], ALU.subtract))
                pool.tensor_copy(table[:, 2, :], left[:, 1, :]).then_inc(table_ready, 1)

        @block.tensor
        def _(pe):
            pe.wait_ge(consts_in, START + 16 * NCONST)
            with pe.Fori(0, N) as i:
                pe.wait_ge(low_ready, START + i + 1)
                pe.wait_ge(rows_ready, START + i)
                for t in range(NT):
                    last = pe.transpose(LT[:, t * 128:(t + 1) * 128], low[:, t * KP:(t + 1) * KP], ident_b[:, :])
                last.then_inc(lt_ready, 1)
                pe.wait_ge(rows_ready, START + i + 1)
                pe.wait_ge(table_ready, START + i + 1)
                for x in range(NT * QUADS + DEEP - 1):
                    if x < NT * QUADS:
                        t, q = x // QUADS, x % QUADS
                        pe.wait_ge(oh_ready, START + i * NT * QUADS + max(x - DEEP + 1, 0))
                        for k in range(q * KQ, min(q * KQ + KQ, K)):
                            last = pe.matmul(BC[:, x % DEEP, (k % KQ) * 128:(k % KQ + 1) * 128], pick_k[:, k, :],
                                             rows[:, t * 128:(t + 1) * 128], start=True, stop=True)
                        last.then_inc(bc_ready, 1)
                    x -= DEEP - 1
                    if x >= 0:
                        t, q = x // QUADS, x % QUADS
                        if q == 0:
                            pe.wait_ge(g_free, START + i * NT + max(t - 1, 0))
                        pe.wait_ge(oh_ready, START + i * NT * QUADS + x + 1)
                        for k in range(q * KQ, min(q * KQ + KQ, K)):
                            half, at_k = (0, k) if k < SPLIT_K else (1, k - SPLIT_K)
                            for part in range(3):
                                last = pe.matmul(G[:, t % 2, half, at_k * 24:at_k * 24 + 24], oh_a[:, x % DEEP, (k % KQ) * 128:(k % KQ + 1) * 128],
                                                 table[:, part, :], start=(part == 0), stop=(part == 2))
                        last.then_inc(fetched, 1)

        @block.scalar
        def _(act):
            def features(f, stage):
                if stage == 0:
                    act.wait_ge(r2_ready, START + f + 1)
                    act.activation(root[:, :, :], r2m[:, :, :], ACT.Sqrt).then_inc(root_ready, 1)
                    act.wait_ge(root_ready, START + f + 1)
                    act.activation(keep["sph"][:, 0:1, bass.ds(f, 1), :], root[:, 0:1, :].unsqueeze(2), ACT.Identity)
                if stage == 1:
                    act.wait_ge(yx_ready, START + f + 1)
                    act.activation(ay[:, :, :], yy[:, :, :], ACT.Abs)
                    act.activation(ax[:, :, :], xx[:, :, :], ACT.Abs).then_inc(abs_ready, 1)
                if stage == 2:
                    act.wait_ge(ratio_ready, START + f + 1)
                    act.activation(at[:, :, :], ratio[:, :, :], ACT.Arctan).then_inc(at_ready, 1)

            def one_hots(i, f):
                act.wait_ge(rows_ready, START + i)
                act.wait_ge(lt_ready, START + i + 1)
                act.activation(low2[:, :], LT[:, :], ACT.Square)
                act.activation(rows[0:32, :], LT[:, :], ACT.Identity).then_inc(lt_copied, 1)
                for x in range(NT * QUADS):
                    cols = (min(KQ, K - (x % QUADS) * KQ)) * 128
                    act.wait_ge(bc_ready, START + i * NT * QUADS + x + 1)
                    act.wait_ge(fetched, START + i * NT * QUADS + max(x - DEEP + 1, 0))
                    act.activation(oh_a[:, x % DEEP, 0:cols], BC[:, x % DEEP, 0:cols], ACT.Relu, scale=-1.0, bias=1.0).then_inc(oh_ready, 1)
                    if f is not None and x in ACT_STAGE:
                        features(f, ACT_STAGE.index(x))

            one_hots(0, None)
            with act.Fori(1, N) as i:
                one_hots(i, i - 1)
            for stage in range(len(ACT_STAGE)):
                features(N - 1, stage)

        @block.vector
        def _(dve):
            dve.memset(rows[96:98, :], 1.0)
            dve.wait_ge(consts_in, START + 16 * NCONST)
            n, base = 0, 0

            def link(ins):
                nonlocal n
                n += 1
                ins.then_inc(dstep, 1)
                dve.wait_ge(dstep, START + base + n)

            def features(f, stage):
                if stage == 0:
                    link(dve.tensor_tensor(sqr[:, :, :], apart[:, :, :], apart[:, :, :], ALU.mult))
                    link(dve.tensor_tensor(r2[:, 1, :], sqr[:, 0, :], sqr[:, 2, :], ALU.add))
                    link(dve.tensor_tensor(r2[:, 0, :], r2[:, 1, :], sqr[:, 1, :], ALU.add))
                    dve.tensor_scalar(r2m[:, :, :], r2[:, :, :], TINY, None, ALU.max).then_inc(r2_ready, 1)
                    link(dve.tensor_scalar(good[:, :, :], r2[:, :, :], TINY, None, ALU.is_ge))
                    link(dve.tensor_scalar(degen[:, :, :], r2[:, :, :], TINY, None, ALU.is_lt))
                if stage == 1:
                    dve.tensor_tensor(yy[:, :, :], apart[:, 1:3, :], good[:, :, :], ALU.mult)
                    dve.wait_ge(root_ready, START + f + 1)
                    link(dve.tensor_tensor(xx[:, 0, :], root[:, 1, :], good[:, 0, :], ALU.mult))
                    link(dve.tensor_tensor(xx[:, 1, :], apart[:, 0, :], good[:, 1, :], ALU.mult))
                    dve.tensor_tensor(xx[:, :, :], xx[:, :, :], degen[:, :, :], ALU.add).then_inc(yx_ready, 1)
                if stage == 2:
                    dve.wait_ge(abs_ready, START + f + 1)
                    link(dve.tensor_tensor(big[:, :, :], ax[:, :, :], ay[:, :, :], ALU.max))
                    link(dve.reciprocal(big[:, :, :], big[:, :, :]))
                    link(dve.tensor_tensor(ratio[:, :, :], ax[:, :, :], ay[:, :, :], ALU.min))
                    dve.tensor_tensor(ratio[:, :, :], ratio[:, :, :], big[:, :, :], ALU.mult).then_inc(ratio_ready, 1)
                    link(dve.tensor_tensor(flag[:, :, :], ay[:, :, :], ax[:, :, :], ALU.is_gt))
                    link(dve.tensor_scalar(turn[:, :, :], flag[:, :, :], -2.0, 1.0, ALU.mult, ALU.add))
                if stage == 3:
                    dve.wait_ge(at_ready, START + f + 1)
                    link(dve.tensor_tensor(at[:, :, :], at[:, :, :], turn[:, :, :], ALU.mult))
                    link(dve.scalar_tensor_tensor(at[:, :, :], flag[:, :, :], float(np.pi / 2), at[:, :, :], ALU.mult, ALU.add))
                    link(dve.tensor_scalar(flag[:, :, :], xx[:, :, :], 0.0, None, ALU.is_lt))
                    link(dve.tensor_scalar(turn[:, :, :], flag[:, :, :], -2.0, 1.0, ALU.mult, ALU.add))
                    link(dve.tensor_tensor(at[:, :, :], at[:, :, :], turn[:, :, :], ALU.mult))
                    link(dve.scalar_tensor_tensor(at[:, :, :], flag[:, :, :], float(np.pi), at[:, :, :], ALU.mult, ALU.add))
                    link(dve.tensor_scalar(flag[:, :, :], yy[:, :, :], 0.0, None, ALU.is_lt))
                    link(dve.tensor_scalar(turn[:, :, :], flag[:, :, :], -2.0, 1.0, ALU.mult, ALU.add))
                    link(dve.tensor_tensor(keep["sph"][:, 1:3, bass.ds(f, 1), :], at[:, :, :].unsqueeze(2), turn[:, :, :].unsqueeze(2), ALU.mult))


            def gather(i, f):
                dve.wait_ge(lt_ready, START + i)
                here = keep["nbr"][:, bass.ds(i, 1), :].rearrange("p u k -> p (u k)")
                link(dve.tensor_copy(high_u[:, :], here))
                link(dve.tensor_scalar(low_u[:, :], high_u[:, :], 127, None, ALU.bitwise_and))
                dve.tensor_copy(low[:, :], low_u[:, :]).then_inc(low_ready, 1)
                link(dve.tensor_scalar(high_u[:, :], high_u[:, :], 7, None, ALU.logical_shift_right))
                link(dve.tensor_copy(high[:, :], high_u[:, :]))
                dve.wait_ge(table_ready, START + i)
                dve.tensor_copy(own[:, :, :].rearrange("p t c -> p (t c)"), keep["pts"][:, bass.ds(i, 1), :].rearrange("p u k -> p (u k)")).then_inc(own_ready, 1)
                link(dve.tensor_tensor(oh_b[:, :, :], high[:, :].unsqueeze(2).to_broadcast([128, NT * KP, 8]),
                                       iota8[:, :].unsqueeze(1).to_broadcast([128, NT * KP, 8]), ALU.is_equal))
                dve.wait_ge(lt_copied, START + i + 1)
                link(dve.tensor_copy(low2_b[:, :], low2[:, :]))
                dve.tensor_copy(rows[32:64, :], low2_b[:, :])
                link(dve.tensor_tensor(rows[64:96, :], low2[:, :], low2_b[:, :], ALU.subtract))
                dve.sem_inc(rows_ready, 1)
                if f is not None:
                    features(f, 0)
                for t in range(NT):
                    dve.wait_ge(fetched, START + (i * NT + t + 1) * QUADS)
                    for half, k0, k1 in ((0, 0, SPLIT_K), (1, SPLIT_K, K)):
                        src = G[:, t % 2, half, 0:(k1 - k0) * 24].rearrange("p (k b c) -> p k b c", b=8, c=3)
                        dst = cand[:, t % 2, k0 * 24:k1 * 24].rearrange("p (k b c) -> p k b c", b=8, c=3)
                        ohs = oh_b[:, t * KP + k0:t * KP + k1, :].unsqueeze(3).to_broadcast([128, k1 - k0, 8, 3])
                        last = dve.tensor_tensor(dst, src, ohs, ALU.mult)
                    last.then_inc(g_free, 1)
                    dve.wait_ge(g_free, START + i * NT + t + 1)
                    last = dve.tensor_reduce(rel[:, :, t, :].rearrange("p c k -> p k c"),
                                             cand[:, t % 2, :].rearrange("p (k b c) -> p k c b", b=8, c=3), AX.X, ALU.add)
                    if f is not None and t in DVE_STAGE:
                        features(f, 1 + DVE_STAGE.index(t))
                link(last)
                link(dve.tensor_tensor(apart[:, :, :].rearrange("p c (t k) -> p c t k", k=K), rel[:, :, :, :],
                                       own[:, :, :].rearrange("p t c -> p c t").unsqueeze(3).to_broadcast([128, 3, NT, K]), ALU.subtract))

            gather(0, None)
            assert n == GATHER_STEPS, n
            with dve.Fori(1, N) as i:
                n, base = 0, GATHER_STEPS + (i - 1) * (GATHER_STEPS + FEATURE_STEPS)
                gather(i, i - 1)
                assert n == GATHER_STEPS + FEATURE_STEPS, n
            n, base = 0, GATHER_STEPS + (N - 1) * (GATHER_STEPS + FEATURE_STEPS)
            for stage in range(1 + len(DVE_STAGE)):
                features(N - 1, stage)


GATHER_STEPS = 9
FEATURE_STEPS = 21
ACT_STAGE = (3, QUADS + 3, 2 * QUADS + 3)
DVE_STAGE = (0, 1, 2)


M_ALL = float(N * T * K)
COLS = N * NF
PIECES = 8
PIECE = COLS // PIECES
SLOPE = 0.2
SERIAL = ["sum1", "all1", "centred", "squares1", "sum_sq1", "all_sq1", "var1", "pow1", "u1",
          "sum2", "all2", "mean2", "squares2", "sum_sq2", "all_sq2", "var2", "pow2", "shift2",
          "sum3", "all3", "mean3", "squares3", "sum_sq3", "all_sq3", "var3", "pow3", "shift3",
          "logit", "less_top", "exp"]


def batch_norms(nc, dram, keep):
    S = keep["sph"][:, :, :, :].rearrange("p c n k -> p c (n k)")
    att = keep["sph"][:, :, :, :].rearrange("p c n k -> p (c n k)")[:, COLS:COLS + N * NT * KP].rearrange("p (m k) -> p m k", k=KP)
    with ExitStack() as es:
        def sb(name, shape, dt=F32):
            return es.enter_context(nc.sbuf_tensor(name, shape, dt))

        def ps(name, shape, dt=F32):
            return es.enter_context(nc.psum_tensor(name, shape, dt))

        def sem(name):
            return es.enter_context(nc.semaphore(name))

        w1 = sb("w1", [128, 6, 6])
        w2 = sb("w2", [128, 3, 6])
        w3 = sb("w3", [128, 3])
        gains = [sb(f"g{n}", [128, w]) for n, w in ((1, 6), (2, 3), (3, 1))]
        shifts = [sb(f"b{n}", [128, w]) for n, w in ((1, 6), (2, 3), (3, 1))]
        ones = sb("c_ones", [128, 128])
        minus_half = sb("minus_half", [128, 6])
        part = sb("part", [128, 6, PIECES])
        partial = sb("partial", [128, 6])
        mean = sb("mean", [128, 3])
        neg_mean = sb("neg_mean", [128, 3])
        cov = sb("cov", [128, 9])
        w1s = sb("w1s", [128, 6])
        v1 = sb("v1", [128, 6, 3])
        vc = sb("vc", [128, 6, 3, 3])
        var = sb("var", [128, 6])
        var_eps = sb("var_eps", [128, 6])
        inv = sb("inv", [128, 6])
        gain = sb("gain", [128, 6])
        shift = sb("shift", [128, 6])
        u1 = sb("u1", [128, 6, 3])
        junk = sb("junk", [128, PIECE])
        junk_a = sb("junk_a", [128, PIECE])
        u = sb("u", [128, 2, PIECE])
        h = sb("h", [128, 2, PIECE])
        p2 = sb("p2", [128, 3, PIECE])
        top = sb("top", [128, N * NT])
        total = sb("total", [128, N * NT])
        SUM = ps("SUM", [128, 16])

        par_in = sem("par_in")
        serial = sem("serial")
        lin = sem("lin")
        lrelued = sem("lrelued")
        used_h = sem("used_h")
        act_g = sem("act_g")
        used_g = sem("used_g")
        dlink = sem("c_dlink")
        plink = sem("c_plink")
        alink = sem("c_alink")
        block = es.enter_context(nc.Block())

        def wait(eng, name):
            eng.wait_ge(serial, SERIAL.index(name) + 1)

        def mark(ins):
            ins.then_inc(serial, 1)

        def piece(x):
            return slice(x * PIECE, (x + 1) * PIECE)

        small = [(w1[:, :, :].rearrange("p a b -> p (a b)"), "W1"), (w2[:, :, :].rearrange("p a b -> p (a b)"), "W2"), (w3[:, :], "W3")]
        small += [(gains[n][:, :], f"g{n + 1}") for n in range(3)] + [(shifts[n][:, :], f"b{n + 1}") for n in range(3)]

        @block.sync
        def _(sp):
            for dst, name in small:
                sp.dma_start(dst, dram[name].broadcast_to([128, dst.shape[1]])).then_inc(par_in, 16)
            sp.wait_ge(par_in, 16 * len(small))

        @block.tensor
        def _(pe):
            for before, name, cols in (("sum1", "all1", 3), ("sum_sq1", "all_sq1", 6), ("sum2", "all2", 3), ("sum_sq2", "all_sq2", 3),
                                       ("sum3", "all3", 1), ("sum_sq3", "all_sq3", 1)):
                wait(pe, before)
                mark(pe.matmul(SUM[:, 0:cols], ones[:, :], partial[:, 0:cols], start=True, stop=True))

        @block.gpsimd
        def _(pool):
            pool.memset(minus_half[:, :], -0.5).then_inc(plink, 1)
            pool.wait_ge(plink, 1)
            n = 1
            for name in ("1", "2", "3"):
                wait(pool, "var" + name)
                pool.tensor_scalar(var_eps[:, :], var[:, :], 1.0, EPS, ALU.mult, ALU.add).then_inc(plink, 1)
                n += 1
                pool.wait_ge(plink, n)
                mark(pool.tensor_tensor(inv[:, :], var_eps[:, :], minus_half[:, :], ALU.pow))

        @block.scalar
        def _(act):
            n = 0

            def squares(width, centre=False):
                nonlocal n
                for c in range(width):
                    for x in range(PIECES):
                        mean_c = {"bias": neg_mean[:, c:c + 1]} if centre else {}
                        last = act.activation(junk_a[:, :], S[:, c, piece(x)], ACT.Square, accum_out=part[:, c, x:x + 1], **mean_c)
                        if (c, x) == (width - 1, PIECES - 1):
                            mark(last)
                        else:
                            n += 1
                            last.then_inc(alink, 1)
                            act.wait_ge(alink, n)

            act.wait_ge(par_in, 16 * len(small))
            wait(act, "centred")
            squares(3)
            wait(act, "u1")
            for y in range(6 * PIECES):
                x, j = y // 6, y % 6
                act.wait_ge(lrelued, max(y - 1, 0))
                act.activation(u[:, y % 2, :], S[:, 0, piece(x)], ACT.Identity, scale=u1[:, j, 0:1], bias=shifts[0][:, j:j + 1]).then_inc(lin, 1)
            wait(act, "mean2")
            squares(3, centre=True)
            wait(act, "shift2")
            for y in range(3 * PIECES):
                x, o = y // 3, y % 3
                act.wait_ge(lrelued, 6 * PIECES + max(y - 1, 0))
                act.activation(u[:, y % 2, :], S[:, o, piece(x)], ACT.Identity, scale=gain[:, o:o + 1], bias=shift[:, o:o + 1]).then_inc(act_g, 1)
            wait(act, "mean3")
            squares(1, centre=True)
            wait(act, "shift3")
            mark(act.activation(S[:, 0, :], S[:, 0, :], ACT.Identity, scale=gain[:, 0:1], bias=shift[:, 0:1]))
            wait(act, "less_top")
            mark(act.activation(S[:, 0, :], S[:, 0, :], ACT.Exp))

        @block.vector
        def _(dve):
            n = 0

            def link(ins):
                nonlocal n
                n += 1
                ins.then_inc(dlink, 1)
                dve.wait_ge(dlink, n)

            link(dve.memset(ones[:, :], 1.0))
            link(dve.memset(var[:, :], 1.0))
            dve.wait_ge(par_in, 16 * len(small))
            link(dve.tensor_reduce(w1s[:, :], w1[:, :, 3:6], AX.X, ALU.add))
            link(dve.tensor_tensor(v1[:, :, :], w1[:, :, 0:3], w1[:, :, 3:6], ALU.add))
            link(dve.scalar_tensor_tensor(v1[:, :, :], w1s[:, :].unsqueeze(2).to_broadcast([128, 6, 3]), -1.0 / 3.0, v1[:, :, :], ALU.mult, ALU.add))
            mark(dve.tensor_reduce(partial[:, 0:3], S, AX.X, ALU.add))
            wait(dve, "all1")
            link(dve.tensor_scalar(mean[:, :], SUM[:, 0:3], 1.0 / M_ALL, None, ALU.mult))
            for c in range(3):
                last = dve.tensor_scalar(S[:, c, :], S[:, c, :], mean[:, c:c + 1], None, ALU.subtract)
            mark(last)
            wait(dve, "centred")
            for m, (a, b) in enumerate(((0, 1), (0, 2), (1, 2))):
                for x in range(PIECES):
                    link(dve.tensor_tensor_reduce(junk[:, :], S[:, a, piece(x)], S[:, b, piece(x)], 1.0, 0.0, ALU.mult, ALU.add,
                                                  part[:, 3 + m, x:x + 1]))
            wait(dve, "squares1")
            mark(dve.tensor_reduce(partial[:, :], part[:, :, :], AX.X, ALU.add))
            wait(dve, "all_sq1")
            scale = 1.0 / M_ALL
            dve.tensor_scalar(cov[:, 0:9:4], SUM[:, 0:3], scale, None, ALU.mult)
            dve.tensor_scalar(cov[:, 1:3], SUM[:, 3:5], scale, None, ALU.mult)
            dve.tensor_scalar(cov[:, 3:7:3], SUM[:, 3:5], scale, None, ALU.mult)
            dve.tensor_scalar(cov[:, 5:6], SUM[:, 5:6], scale, None, ALU.mult)
            link(dve.tensor_scalar(cov[:, 7:8], SUM[:, 5:6], scale, None, ALU.mult))
            full = [128, 6, 3, 3]
            link(dve.tensor_tensor(vc[:, :, :, :], v1[:, :, :].unsqueeze(3).to_broadcast(full),
                                   cov[:, :].rearrange("p (a b) -> p a b", a=3).unsqueeze(1).to_broadcast(full), ALU.mult))
            link(dve.tensor_tensor(vc[:, :, :, :], vc[:, :, :, :], v1[:, :, :].unsqueeze(2).to_broadcast(full), ALU.mult))
            mark(dve.tensor_reduce(var[:, :], vc[:, :, :, :].rearrange("p j a b -> p j (a b)"), AX.X, ALU.add))
            wait(dve, "pow1")
            link(dve.tensor_tensor(gain[:, :], inv[:, :], gains[0][:, :], ALU.mult))
            mark(dve.tensor_tensor(u1[:, :, :], v1[:, :, :], gain[:, :].unsqueeze(2).to_broadcast([128, 6, 3]), ALU.mult))
            wait(dve, "u1")
            for y in range(6 * PIECES + 1):
                x, j = y // 6, y % 6
                if y < 6 * PIECES:
                    dve.wait_ge(lin, y + 1)
                    link(dve.scalar_tensor_tensor(u[:, y % 2, :], S[:, 1, piece(x)], u1[:, j, 1:2], u[:, y % 2, :], ALU.mult, ALU.add))
                    link(dve.scalar_tensor_tensor(u[:, y % 2, :], S[:, 2, piece(x)], u1[:, j, 2:3], u[:, y % 2, :], ALU.mult, ALU.add))
                    dve.scalar_tensor_tensor(h[:, y % 2, :], u[:, y % 2, :], SLOPE, u[:, y % 2, :], ALU.mult, ALU.max).then_inc(lrelued, 1)
                y -= 1
                x, j = y // 6, y % 6
                if y >= 0:
                    dve.wait_ge(lrelued, y + 1)
                    if y:
                        dve.wait_ge(used_h, y)
                    for o in range(3):
                        dst = S[:, o, piece(x)] if j == 5 else p2[:, o, :]
                        if j == 0:
                            last = dve.tensor_scalar(dst, h[:, y % 2, :], w2[:, o, j:j + 1], None, ALU.mult)
                        else:
                            last = dve.scalar_tensor_tensor(dst, h[:, y % 2, :], w2[:, o, j:j + 1], p2[:, o, :], ALU.mult, ALU.add)
                    last.then_inc(used_h, 1)
            dve.wait_ge(used_h, 6 * PIECES)

            def norm(name, width):
                mark(dve.tensor_reduce(partial[:, 0:width], S[:, 0:width, :], AX.X, ALU.add))
                wait(dve, "all" + name)
                mark(dve.tensor_scalar(neg_mean[:, 0:width], SUM[:, 0:width], -1.0 / M_ALL, None, ALU.mult))
                wait(dve, "squares" + name)
                mark(dve.tensor_reduce(partial[:, 0:width], part[:, 0:width, :], AX.X, ALU.add))
                wait(dve, "all_sq" + name)
                mark(dve.tensor_scalar(var[:, 0:width], SUM[:, 0:width], 1.0 / M_ALL, None, ALU.mult))
                wait(dve, "pow" + name)
                g, b = gains[int(name) - 1], shifts[int(name) - 1]
                link(dve.tensor_tensor(gain[:, 0:width], inv[:, 0:width], g[:, 0:width], ALU.mult))
                link(dve.tensor_tensor(shift[:, 0:width], neg_mean[:, 0:width], gain[:, 0:width], ALU.mult))
                mark(dve.tensor_tensor(shift[:, 0:width], shift[:, 0:width], b[:, 0:width], ALU.add))

            norm("2", 3)
            for y in range(3 * PIECES):
                x, o = y // 3, y % 3
                dve.wait_ge(act_g, y + 1)
                dve.scalar_tensor_tensor(h[:, y % 2, :], u[:, y % 2, :], SLOPE, u[:, y % 2, :], ALU.mult, ALU.max).then_inc(lrelued, 1)
                dve.wait_ge(lrelued, 6 * PIECES + y + 1)
                if y:
                    dve.wait_ge(used_g, y)
                if o == 0:
                    last = dve.tensor_scalar(S[:, 0, piece(x)], h[:, y % 2, :], w3[:, o:o + 1], None, ALU.mult)
                else:
                    last = dve.scalar_tensor_tensor(S[:, 0, piece(x)], h[:, y % 2, :], w3[:, o:o + 1], S[:, 0, piece(x)], ALU.mult, ALU.add)
                last.then_inc(used_g, 1)
            dve.wait_ge(used_g, 3 * PIECES)
            norm("3", 1)
            dve.memset(att[:, :, K:KP], 0.0)
            wait(dve, "logit")
            link(dve.scalar_tensor_tensor(S[:, 0, :], S[:, 0, :], SLOPE, S[:, 0, :], ALU.mult, ALU.max))
            logit = S[:, 0, :].rearrange("p (m k) -> p m k", k=K)
            wide = [128, N * NT, K]
            link(dve.tensor_reduce(top[:, :], logit, AX.X, ALU.max))
            mark(dve.tensor_tensor(logit, logit, top[:, :].unsqueeze(2).to_broadcast(wide), ALU.subtract))
            wait(dve, "exp")
            link(dve.tensor_reduce(total[:, :], logit, AX.X, ALU.add))
            link(dve.reciprocal(total[:, :], total[:, :]))
            link(dve.tensor_tensor(att[:, :, 0:K], logit, total[:, :].unsqueeze(2).to_broadcast(wide), ALU.mult))
    keep["att"] = att


GROUPS = 32
LAG_E = 1


def neighbour_sum(nc, dram, keep):
    with ExitStack() as es:
        def sb(name, shape, dt=F32):
            return es.enter_context(nc.sbuf_tensor(name, shape, dt))

        def ps(name, shape, dt=F32):
            return es.enter_context(nc.psum_tensor(name, shape, dt))

        counts = []

        def sem(name):
            counts.append(es.enter_context(nc.semaphore(name)))
            return counts[-1]

        ident = sb("d_ident", [128, 128])
        iota_a = sb("iota_a", [128, 128, GROUPS], BF16)
        iota_j = sb("iota_j", [128, 32, GROUPS], BF16)
        eight_q = sb("eight_q", [128, 1])
        minus_half = sb("d_minus_half", [128, 1])
        nb = sb("nb", [128, NT * KP], U16)
        nb_t = sb("nb_t", [128, NT * KP], U16)
        lo_u = sb("lo_u", [128, NT * KP], U16)
        hi_u = sb("hi_u", [128, NT * KP], U16)
        lo = sb("lo", [128, NT, GROUPS], BF16)
        hj = sb("hj", [128, NT, GROUPS], BF16)
        at_n = sb("at_n", [128, NT * KP])
        at_t = sb("at_t", [128, NT * KP])
        rest = sb("d_rest", [128, 2, NT * KP])
        at3 = sb("at3", [128, 3, NT, GROUPS], BF16)
        oh_a = sb("d_oh_a", [128, 2, 128, GROUPS], BF16)
        oh_j = sb("oh_j", [128, 2, 32, GROUPS], BF16)
        placed = sb("placed", [128, 2, 3, 32, GROUPS], BF16)
        x2 = sb("d_x2", [128, BPD, T])
        y3 = sb("d_y3", [128, BPD, T])
        x2_t = sb("x2_t", [128, NT, 128])
        dense = sb("dense", [128, 8, HALF])
        y = sb("d_y", [128, BPD, T])
        stats = sb("d_stats", [128, 2, 6])
        moments = sb("d_moments", [128, 2])
        rstd = sb("d_rstd", [128, 3])

        DM = ps("DM", [128, 2, 512])
        XT = ps("XT", [128, 2, 512])
        AG = ps("AG", [128, 2, 512])

        consts_in = sem("d_consts_in")
        x2_in = [sem(f"x2_in{u}") for u in range(BPD)]
        y3_in = [sem(f"y3_in{u}") for u in range(BPD)]
        copied_in = sem("copied_in")
        split = sem("d_split")
        at_ready = sem("d_at_ready")
        at3_ready = sem("at3_ready")
        oh_ready = sem("d_oh_ready")
        placed_ready = sem("placed_ready")
        low_placed = sem("low_placed")
        oh_j_ready = sem("oh_j_ready")
        dense_ready = sem("dense_ready")
        dense_copied = sem("dense_copied")
        xt_ready = sem("xt_ready")
        xt_copied = sem("xt_copied")
        summed = sem("summed")
        read_out = sem("read_out")
        y3_added = sem("y3_added")
        moments_ready = sem("d_moments_ready")
        pool_ln = sem("d_pool_ln")
        rstd_ready = sem("d_rstd_ready")
        normed = sem("d_normed")
        out_done = [sem(f"out_done{u}") for u in range(BPD)]
        dstep = sem("d_dstep")
        passed = sem("d_passed")
        CONSTS = [(ident[:, :], "ident"), (iota_a[:, :, :], "iota_a"), (iota_j[:, :, :], "iota_j"), (eight_q[:, :], "eight_q"),
                  (minus_half[:, :], "pow_half")]
        block = es.enter_context(nc.Block())

        @block.sync
        def _(sp):
            for dst, name in CONSTS:
                sp.dma_start(dst, dram[name]).then_inc(consts_in, 16)
            with sp.Fori(0, BODY_D) as i:
                for u in range(BPD):
                    sp.wait_ge(out_done[u], START + i * 16)
                    sp.dma_start(x2[:, u, :], dram["x2"][i * BPD + u]).then_inc(x2_in[u], 16)
                    sp.dma_start(y3[:, u, :], dram["y3"][i * BPD + u]).then_inc(y3_in[u], 16)

        @block.tensor
        def _(pe):
            pe.wait_ge(consts_in, START + 16 * len(CONSTS))
            with pe.Fori(0, BODY_D) as i:
                for u in range(BPD):
                    def b(n, k=0):
                        return (i * BPD + u) * n + k

                    pe.wait_ge(x2_in[u], START + (i + 1) * 16)
                    pe.wait_ge(xt_copied, START + b(1))
                    for t in range(NT):
                        last = pe.transpose(XT[:, t // 4, (t % 4) * 128:(t % 4 + 1) * 128], x2[:, u, t * 128:(t + 1) * 128], ident[:, :])
                    last.then_inc(xt_ready, 1)
                    for hh in range(2):
                        for t in range(4 * hh, 4 * hh + 4):
                            pe.wait_ge(oh_ready, START + b(NT, t + 1))
                            pe.wait_ge(placed_ready, START + b(NT, t + 1))
                            pe.wait_ge(low_placed, START + b(NT, t + 1))
                            for e in range(2):
                                pe.wait_ge(dense_copied, START + (b(2 * NT, 2 * t + e - 1) if (t or e or u) else i * BPD * 2 * NT))
                                for g in range(16 * e, 16 * e + 16):
                                    for part in range(3):
                                        last = pe.matmul(DM[:, e, (g % 16) * 32:(g % 16 + 1) * 32], oh_a[:, t % 2, :, g],
                                                         placed[:, t % 2, part, :, g], start=(part == 0), stop=(part == 2))
                                last.then_inc(dense_ready, 1)
                        if hh == 0:
                            pe.wait_ge(xt_copied, START + b(1, 1))
                        pe.wait_ge(dense_copied, START + b(2 * NT, 8 * hh + 8))
                        pe.wait_ge(read_out, START + (b(2, hh - 1) if (hh or u) else i * BPD * 2))
                        for m in range(8):
                            last = pe.matmul(AG[:, hh, :], x2_t[:, m, :], dense[:, m, :], start=(m == 0), stop=(m == 7))
                        last.then_inc(summed, 1)

        @block.scalar
        def _(act):
            with act.Fori(0, BODY_D) as i:
                for u in range(BPD):
                    def b(n, k=0):
                        return (i * BPD + u) * n + k

                    act.wait_ge(at_ready, START + b(1))
                    act.activation(at_n[:, :].rearrange("p (n k) -> p n k", k=KP), keep["att"][:, bass.ds((i * BPD + u) * NT, NT), :],
                                   ACT.Identity).then_inc(copied_in, 1)
                    act.wait_ge(xt_ready, START + b(1, 1))
                    act.wait_ge(summed, START + b(2))
                    act.activation(x2_t[:, :, :].rearrange("p t c -> p (t c)"), flat(XT[:, :, :]), ACT.Identity).then_inc(xt_copied, 1)
                    for x in range(2 * NT):
                        t, e = x // 2, x % 2
                        act.wait_ge(dense_ready, START + b(2 * NT, x + 1))
                        if x in (0, NT):
                            act.wait_ge(summed, START + b(2, x // NT))
                        src = DM[:, e, :].rearrange("p (g q m) -> p g q m", q=4, m=8)
                        at0 = (t % 4) * 128 + e * 64
                        dst = dense[:, :, at0:at0 + 64].rearrange("p m (g q) -> p g q m", q=4)
                        act.activation(dst, src, ACT.Identity).then_inc(dense_copied, 1)
                    act.wait_ge(rstd_ready, START + b(1, 1))
                    act.activation(y[:, u, :], y[:, u, :], ACT.Identity, scale=rstd[:, 1:2], bias=rstd[:, 2:3]).then_inc(normed, 1)
                    act.wait_ge(normed, START + b(1, 1))
                    act.dma_start(dram["out"][i * BPD + u], y[:, u, :]).then_inc(out_done[u], 16)
            for u in range(BPD):
                act.wait_ge(out_done[u], START + BODY_D * 16)

        @block.gpsimd
        def _(pool):
            start_counts(pool, counts)
            with pool.Fori(0, BODY_D) as i:
                n = 0

                def then(ins, plain=True):
                    nonlocal n
                    n += 1
                    ins.then_inc(split, 1)
                    pool.wait_ge(split, START + i * 6 * BPD + n)
                    pool.sem_inc(passed, 1)

                for u in range(BPD):
                    def b(n, k=0):
                        return (i * BPD + u) * n + k

                    flat3 = at3[:, :, :, :].rearrange("p s t g -> p s (t g)")
                    pool.wait_ge(at_ready, START + b(1, 1))
                    pool.wait_ge(placed_ready, START + b(NT))
                    pool.sem_inc(passed, 1)
                    then(pool.tensor_copy(flat3[:, 0, :], at_t[:, :]))
                    then(pool.tensor_tensor(rest[:, 0, :], at_t[:, :], flat3[:, 0, :], ALU.subtract))
                    then(pool.tensor_copy(flat3[:, 1, :], rest[:, 0, :]))
                    then(pool.tensor_tensor(rest[:, 1, :], rest[:, 0, :], flat3[:, 1, :], ALU.subtract))
                    pool.tensor_copy(flat3[:, 2, :], rest[:, 1, :]).then_inc(at3_ready, 1)
                    pool.wait_ge(at3_ready, START + b(1, 1))
                    pool.wait_ge(y3_in[u], START + (i + 1) * 16)
                    for t in range(NT):
                        pool.wait_ge(oh_j_ready, START + b(NT, t + 1))
                        pool.wait_ge(dense_ready, START + (b(2 * NT, 2 * (t - 1)) if (t or u) else i * BPD * 2 * NT))
                        pool.tensor_tensor(placed[:, t % 2, 2, :, :], oh_j[:, t % 2, :, :],
                                           at3[:, 2, t:t + 1, :].to_broadcast([128, 32, GROUPS]), ALU.mult).then_inc(low_placed, 1)
                        if t in (4 + LAG_E, NT - 1):
                            hh = 0 if t < NT - 1 else 1
                            pool.wait_ge(read_out, START + b(2, hh + 1))
                            half = slice(hh * HALF, (hh + 1) * HALF)
                            pool.tensor_tensor(y[:, u, half], y[:, u, half], y3[:, u, half], ALU.add).then_inc(y3_added, 1)
                    pool.wait_ge(moments_ready, START + b(1, 1))
                    pool.wait_ge(normed, START + b(1))
                    pool.sem_inc(passed, 1)
                    then(pool.tensor_scalar(rstd[:, 0:1], moments[:, 1:2], 1.0, EPS, ALU.mult, ALU.add))
                    then(pool.tensor_tensor(rstd[:, 1:2], rstd[:, 0:1], minus_half[:, :], ALU.pow))
                    pool.tensor_scalar(rstd[:, 2:3], moments[:, 0:1], rstd[:, 1:2], -1.0, ALU.mult, ALU.mult).then_inc(rstd_ready, 1)

        @block.vector
        def _(dve):
            dve.wait_ge(consts_in, START + 16 * len(CONSTS))
            with dve.Fori(0, BODY_D) as i:
                n = 0

                def link(ins, plain=False):
                    nonlocal n
                    n += 1
                    ins.then_inc(dstep, 1)
                    dve.wait_ge(dstep, START + i * D_STEPS + n)
                    if plain:
                        dve.sem_inc(passed, 1)

                for u in range(BPD):
                    def b(n, k=0):
                        return (i * BPD + u) * n + k

                    link(dve.tensor_copy(nb[:, :], keep["nbr"][:, bass.ds(i * BPD + u, 1), :].rearrange("p u k -> p (u k)")))
                    link(dve.transpose(nb_t[:, :], nb[:, :]))
                    link(dve.tensor_scalar(lo_u[:, :], nb_t[:, :], 127, None, ALU.bitwise_and))
                    link(dve.tensor_scalar(hi_u[:, :], nb_t[:, :], 7, None, ALU.logical_shift_right))
                    dve.tensor_copy(lo[:, :, :].rearrange("p t g -> p (t g)"), lo_u[:, :])
                    link(dve.tensor_scalar(hj[:, :, :].rearrange("p t g -> p (t g)"), hi_u[:, :], eight_q[:, 0:1], None, ALU.add))
                    dve.wait_ge(copied_in, START + b(1, 1))
                    dve.wait_ge(at3_ready, START + b(1))
                    dve.transpose(at_t[:, :], at_n[:, :]).then_inc(at_ready, 1)
                    for t in range(NT + 1):
                        if t < NT:
                            dve.wait_ge(dense_ready, START + (b(2 * NT, 2 * (t - 1)) if (t or u) else i * BPD * 2 * NT))
                            wide = [128, 128, GROUPS]
                            dve.tensor_tensor(oh_a[:, t % 2, :, :], lo[:, t:t + 1, :].to_broadcast(wide), iota_a[:, :, :], ALU.is_equal).then_inc(oh_ready, 1)
                            wide = [128, 32, GROUPS]
                            dve.tensor_tensor(oh_j[:, t % 2, :, :], hj[:, t:t + 1, :].to_broadcast(wide), iota_j[:, :, :], ALU.is_equal).then_inc(oh_j_ready, 1)
                            dve.wait_ge(oh_j_ready, START + b(NT, t + 1))
                            if t == 0:
                                dve.wait_ge(at3_ready, START + b(1, 1))
                            for part in range(2):
                                last = dve.tensor_tensor(placed[:, t % 2, part, :, :], oh_j[:, t % 2, :, :],
                                                         at3[:, part, t:t + 1, :].to_broadcast(wide), ALU.mult)
                            last.then_inc(placed_ready, 1)
                        if t in (4 + LAG_E, NT):
                            hh = 0 if t < NT else 1
                            dve.wait_ge(summed, START + b(2, hh + 1))
                            if hh == 0:
                                dve.wait_ge(out_done[u], START + i * 16)
                            half = slice(hh * HALF, (hh + 1) * HALF)
                            view = "p (t q g) -> p t g q"
                            dve.tensor_tensor(y[:, u, half].rearrange(view, q=4, g=GROUPS), AG[:, hh, :].rearrange("p (t g q) -> p t g q", q=4, g=GROUPS),
                                              x2[:, u, half].rearrange(view, q=4, g=GROUPS), ALU.add).then_inc(read_out, 1)
                    dve.wait_ge(y3_added, START + b(2, 2))
                    dve.bn_stats(stats[:, 0, :], y[:, u, 0:HALF])
                    link(dve.bn_stats(stats[:, 1, :], y[:, u, HALF:T]))
                    dve.wait_ge(rstd_ready, START + b(1))
                    dve.sem_inc(passed, 1)
                    dve.bn_aggr(moments[:, :], stats[:, :, :]).then_inc(moments_ready, 1)
                assert n == D_STEPS, n


D_STEPS = BPD * (5 + 1)


def build(nc, dram):
    with ExitStack() as es:
        keep = {"nbr": es.enter_context(nc.sbuf_tensor("nbr_all", [128, N, NT * KP], U16)),
                "pts": es.enter_context(nc.sbuf_tensor("pts_all", [128, N, 3 * NT], F32))}
        attention_and_neighbours(nc, dram, keep)
        keep["sph"] = es.enter_context(nc.sbuf_tensor("sph_all", [128, 3, N, NF], F32))
        spherical_features(nc, dram, keep)
        batch_norms(nc, dram, keep)
        neighbour_sum(nc, dram, keep)


def high_bits(a):
    return (np.asarray(a, np.float32).view(np.uint32) >> 16).astype(np.uint16)


def widened(bits):
    return (np.asarray(bits).astype(np.uint32) << 16).view(np.float32)


def constants():
    out = {"ident": np.eye(128, dtype=np.float32)}
    hm = np.zeros((C, 4, 2), np.float32)
    for c in range(C):
        h = c // DH
        hm[c, 2 * (h // 4) + h % 2, (h // 2) % 2] = DH ** -0.5
    out["head_mask"] = hm.reshape(C, 8)
    pick = np.zeros((96, 128), np.float32)
    pick[[0, 32, 64]] = 1.0
    out["pick3"] = high_bits(pick)
    out["ones3"] = high_bits(np.ones((3, 128)))
    left, parts = np.float32(-1e9), []
    for _ in range(3):
        parts.append(widened(high_bits(left)))
        left = left - parts[-1]
    assert left == 0
    out["neg3"] = np.array(parts, np.float32).reshape(3, 1)
    out["half_neg"] = np.full((128, 128), -0.5, np.float32)
    out["pow_half"] = np.full((128, 1), -0.5, np.float32)
    out["perm3"] = np.eye(128, dtype=np.float32)[:, [0, 2, 1]]
    out["ident_b"] = high_bits(np.eye(128))
    a = np.arange(128)
    pk = np.zeros((98, K, 128), np.float32)
    high_sq = widened(high_bits(a * a))
    for k in range(K):
        pk[k, k] = -2.0 * a
        pk[32 + k, k] = 1.0
        pk[64 + k, k] = 1.0
        pk[96, k] = high_sq
        pk[97, k] = a * a - high_sq
    out["pick_k"] = high_bits(pk)
    out["iota8"] = np.tile(np.arange(8, dtype=np.float32), (128, 1))
    out["iota_a"] = high_bits(np.tile(np.arange(128, dtype=np.float32)[None, :, None], (128, 1, 32)))
    out["iota_j"] = high_bits(np.tile(np.arange(32, dtype=np.float32)[None, :, None], (128, 1, 32)))
    out["eight_q"] = (8 * (np.arange(128, dtype=np.float32) // 32)).reshape(128, 1)
    return out


_LAYER_NAMES = ["L0_xattn", "L1_xattn", "L3_xattn"]


def kernel(**inputs):
    import concourse.bacc as _bacc
    from concourse.bass_utils import run_bass_kernel_spmd as _run

    nc = _bacc.Bacc("TRN2", target_bir_lowering=False, num_devices=1)
    arrays, dram = {}, {}

    def given(name, a):
        a = np.ascontiguousarray(a)
        arrays[f"in_{name}"] = a
        return nc.dram_tensor(f"in_{name}", a.shape, mybir.dt.from_np(a.dtype), kind="ExternalInput").ap()

    dram["x"] = given("x", inputs["x"])
    dram["ctx"] = given("ctx", inputs["ctx_4096"])
    dram["mask"] = given("mask", inputs["mask_Bx1x4096_ff1"])
    dram["w_in"] = [given(f"{l}_w_in", np.asarray(inputs[f"{l}_W_in"]).T) for l in _LAYER_NAMES]
    dram["w_out"] = [given(f"{l}_w_out", np.asarray(inputs[f"{l}_W_out"]).T) for l in _LAYER_NAMES]
    dram["b_in"] = [given(f"{l}_b_in", np.asarray(inputs[f"{l}_b_in"]).reshape(3, C).T) for l in _LAYER_NAMES]
    dram["b_out"] = [given(f"{l}_b_out", np.asarray(inputs[f"{l}_b_out"]).reshape(C, 1)) for l in _LAYER_NAMES]
    for name in ("W1", "W2", "W3", "g1", "g2", "g3", "b1", "b2", "b3"):
        dram[name] = given(name, np.asarray(inputs[f"L2_xattn_{name}"]).reshape(1, -1))
    for name, a in constants().items():
        dram[name] = given(name, a)
        if a.dtype == np.uint16:
            dram[name] = dram[name].bitcast(BF16)
    dram["x2"] = nc.dram_tensor("x2_scratch", (N, C, T), F32, kind="Internal").ap()
    dram["y3"] = nc.dram_tensor("y3_scratch", (N, C, T), F32, kind="Internal").ap()
    dram["out"] = nc.dram_tensor("out", (N, C, T), F32, kind="ExternalOutput").ap()
    build(nc, dram)
    r = _run(nc, [arrays], core_ids=[0])
    return r.results[0]["out"]
```
